# Optimizing a Trainium2 kernel written in Bass

```python
import numpy as np
import jax
import jax.numpy as jnp

def _softmax(x, axis=-1):
    return jax.nn.softmax(x, axis=axis)

def _gelu(x):
    return jax.nn.gelu(x, approximate=True)

def _silu(x):
    return jax.nn.silu(x)

def _sigmoid(x):
    return jax.nn.sigmoid(x)

def _layernorm(x, axis=-1, eps=1e-05):
    m = jnp.mean(x, axis=axis, keepdims=True)
    v = jnp.var(x, axis=axis, keepdims=True)
    return (x - m) / jnp.sqrt(v + eps)

def _scatter_add(tgt, idx, src, axis=0):
    return tgt.at[idx].add(src)

def _segment_sum(src, seg, n):
    return jax.ops.segment_sum(src, seg, n)
kernel_name = 'mk_xattn_ffn_d1_seqx_r4_3f722a'

def setup_inputs(seed: int=0):
    np.random.seed(seed)
    _w = jnp.asarray

    def _rec_inputs():
        import jax
        import jax.numpy as jnp
        _rk = jax.random.key(seed)
        x = -0.0002928 + 1 * jax.random.normal(jax.random.fold_in(_rk, 1), (4, 512, 256), jnp.float32)
        _lenS = 512 - jax.random.randint(jax.random.fold_in(_rk, 7), (4,), 0, max(1, 512 // 4) + 1, jnp.int32)
        _lenS2 = 512 - jax.random.randint(jax.random.fold_in(_rk, 8), (4,), 0, max(1, 512 // 4) + 1, jnp.int32)
        _ctx_1024P = jax.random.normal(jax.random.fold_in(_rk, 11), (4, 16, 256), jnp.float32)
        _ctx_1024c = jax.random.dirichlet(jax.random.fold_in(_rk, 511), 0.3 * jnp.ones((16,), jnp.float32), (4, 512))
        _ctx_1024t = jnp.einsum('bsk,bkd->bsd', _ctx_1024c, _ctx_1024P)
        _ctx_1024t = _ctx_1024t * jax.lax.rsqrt(jnp.mean(jnp.square(_ctx_1024t)) + 1e-12) * 0.953939
        ctx_1024 = -1.39393e-06 + 0.999914 * (_ctx_1024t + 0.3 * jax.random.normal(jax.random.fold_in(_rk, 611), (4, 512, 256), jnp.float32))
        return (x, ctx_1024)
    x, ctx_1024 = _rec_inputs()

    def _L0_xattn_setup():
        import jax, jax.numpy as jnp
        import numpy as np
        EMB = 256
        NH = 8
        HD = EMB // NH
        EPS = 1e-06

        def _mlstm_head(q, k, v, ig, fg):
            S, DH = q.shape
            log_fg = jax.nn.log_sigmoid(fg)
            cs = jnp.concatenate([jnp.zeros((1, 1), q.dtype), jnp.cumsum(log_fg, axis=0)], axis=0)
            fg_mat_full = cs - cs.T
            ltr = jnp.tril(jnp.ones((S, S), bool))
            log_fg_matrix = jnp.where(ltr, fg_mat_full[1:, 1:], -jnp.inf)
            log_D = log_fg_matrix + ig.T
            max_log_D = jnp.max(log_D, axis=-1, keepdims=True)
            D = jnp.exp(log_D - max_log_D)
            qk = q @ (k.T / jnp.sqrt(jnp.asarray(DH, q.dtype)))
            C = qk * D
            normalizer = jnp.maximum(jnp.abs(C.sum(-1, keepdims=True)), jnp.exp(-max_log_D))
            return C / (normalizer + EPS) @ v
        key = jax.random.key(seed)
        ks = jax.random.split(key, 6)
        B, S = (2, 512)
        q = jax.random.normal(ks[0], (B, S, EMB), jnp.float32)
        k = jax.random.normal(ks[1], (B, S, EMB), jnp.float32)
        v = jax.random.normal(ks[2], (B, S, EMB), jnp.float32)
        igate_kernel = jax.random.normal(ks[3], (3 * EMB, NH), jnp.float32) * 0.02
        igate_bias = jax.random.normal(ks[4], (NH,), jnp.float32) * 0.1
        fgate_kernel = jax.random.normal(ks[5], (3 * EMB, NH), jnp.float32) * 0.02
        fgate_bias = jnp.linspace(3.0, 6.0, NH).astype(jnp.float32)
        return dict(q=q, k=k, v=v, igate_kernel=igate_kernel, igate_bias=igate_bias, fgate_kernel=fgate_kernel, fgate_bias=fgate_bias)
    _L0_xattn_all = _L0_xattn_setup()
    _L0_xattn_in = {k: v for k, v in _L0_xattn_all.items() if k in ('igate_kernel', 'igate_bias', 'fgate_kernel', 'fgate_bias')}
    del _L0_xattn_all

    def _L0_ffn_setup():
        import math
        import jax, jax.numpy as jnp
        import numpy as np
        CAPACITY_FACTOR = 1.25
        key = jax.random.key(seed)
        ks = jax.random.split(key, 5)
        B, S, H, F, E = (4, 1024, 256, 256, 32)
        scale_in = 1.0 / math.sqrt(H)
        scale_mid = 1.0 / math.sqrt(F)
        return {'x': jax.random.normal(ks[0], (B, S, H), dtype=jnp.float32), 'w_router': jax.random.normal(ks[1], (H, E), dtype=jnp.float32) * scale_in, 'w_gate': jax.random.normal(ks[2], (E, H, F), dtype=jnp.float32) * scale_in, 'w_up': jax.random.normal(ks[3], (E, H, F), dtype=jnp.float32) * scale_in, 'w_down': jax.random.normal(ks[4], (E, F, H), dtype=jnp.float32) * scale_mid}
    _L0_ffn_all = _L0_ffn_setup()
    _L0_ffn_in = {k: v for k, v in _L0_ffn_all.items() if k in ('w_router', 'w_gate', 'w_up', 'w_down')}
    del _L0_ffn_all
    return {'x': x, 'ctx_1024': ctx_1024, 'L0_xattn_igate_kernel': _L0_xattn_in['igate_kernel'], 'L0_xattn_igate_bias': _L0_xattn_in['igate_bias'], 'L0_xattn_fgate_kernel': _L0_xattn_in['fgate_kernel'], 'L0_xattn_fgate_bias': _L0_xattn_in['fgate_bias'], 'L0_ffn_w_router': _L0_ffn_in['w_router'], 'L0_ffn_w_gate': _L0_ffn_in['w_gate'], 'L0_ffn_w_up': _L0_ffn_in['w_up'], 'L0_ffn_w_down': _L0_ffn_in['w_down']}

def reference(x, ctx_1024, L0_xattn_igate_kernel, L0_xattn_igate_bias, L0_xattn_fgate_kernel, L0_xattn_fgate_bias, L0_ffn_w_router, L0_ffn_w_gate, L0_ffn_w_up, L0_ffn_w_down):
    import jax
    import jax.numpy as jnp

    def _L0_xattn_ref(q, k, v, igate_kernel, igate_bias, fgate_kernel, fgate_bias):
        import jax, jax.numpy as jnp
        import numpy as np
        EMB = 256
        NH = 8
        HD = EMB // NH
        EPS = 1e-06

        def _mlstm_head(q, k, v, ig, fg):
            S, DH = q.shape
            log_fg = jax.nn.log_sigmoid(fg)
            cs = jnp.concatenate([jnp.zeros((1, 1), q.dtype), jnp.cumsum(log_fg, axis=0)], axis=0)
            fg_mat_full = cs - cs.T
            ltr = jnp.tril(jnp.ones((S, S), bool))
            log_fg_matrix = jnp.where(ltr, fg_mat_full[1:, 1:], -jnp.inf)
            log_D = log_fg_matrix + ig.T
            max_log_D = jnp.max(log_D, axis=-1, keepdims=True)
            D = jnp.exp(log_D - max_log_D)
            qk = q @ (k.T / jnp.sqrt(jnp.asarray(DH, q.dtype)))
            C = qk * D
            normalizer = jnp.maximum(jnp.abs(C.sum(-1, keepdims=True)), jnp.exp(-max_log_D))
            return C / (normalizer + EPS) @ v
        B, S, H = q.shape
        x = jnp.concatenate([q, k, v], axis=-1)
        ig = x @ igate_kernel + igate_bias
        fg = x @ fgate_kernel + fgate_bias
        qh = q.reshape(B, S, NH, HD).swapaxes(1, 2)
        kh = k.reshape(B, S, NH, HD).swapaxes(1, 2)
        vh = v.reshape(B, S, NH, HD).swapaxes(1, 2)
        igp = ig.swapaxes(1, 2)[..., None]
        fgp = fg.swapaxes(1, 2)[..., None]
        h = jax.vmap(jax.vmap(_mlstm_head))(qh, kh, vh, igp, fgp)
        hf = h.astype(jnp.float32)
        h = (hf * jax.lax.rsqrt(jnp.mean(jnp.square(hf), axis=-1, keepdims=True) + 1e-06)).astype(h.dtype)
        return h.swapaxes(1, 2).reshape(B, S, H)

    def _L0_ffn_ref(x, w_router, w_gate, w_up, w_down):
        import math
        import jax, jax.numpy as jnp
        import numpy as np
        CAPACITY_FACTOR = 1.25
        B, S, H = x.shape
        E = w_gate.shape[0]
        T = B * S
        C = int(math.ceil(CAPACITY_FACTOR * T / E))
        xt = x.reshape(T, H)
        logits = xt @ w_router
        probs = jax.nn.softmax(logits, axis=-1)
        top1 = jnp.argmax(probs, axis=-1)
        gate = jnp.take_along_axis(probs, top1[:, None], axis=1)[:, 0]
        onehot = jax.nn.one_hot(top1, E, dtype=jnp.int32)
        pos = jnp.cumsum(onehot, axis=0)[jnp.arange(T), top1] - 1
        accepted = pos < C
        slot = jnp.where(accepted, top1 * C + pos, E * C)
        buf = jnp.zeros((E * C + 1, H), dtype=x.dtype).at[slot].set(xt)
        buf = buf[:E * C].reshape(E, C, H)
        g = jnp.einsum('ech,ehf->ecf', buf, w_gate)
        u = jnp.einsum('ech,ehf->ecf', buf, w_up)
        y = jnp.einsum('ecf,efh->ech', jax.nn.silu(g) * u, w_down)
        out_tok = y.reshape(E * C, H)[jnp.clip(slot, 0, E * C - 1)]
        out_tok = jnp.where(accepted[:, None], out_tok * gate[:, None], 0.0)
        return (xt + out_tok).reshape(B, S, H)
    x = x + _L0_xattn_ref(_layernorm(x, axis=-1), ctx_1024, ctx_1024, L0_xattn_igate_kernel, L0_xattn_igate_bias, L0_xattn_fgate_kernel, L0_xattn_fgate_bias)
    x = x + _L0_ffn_ref(_layernorm(x, axis=-1), L0_ffn_w_router, L0_ffn_w_gate, L0_ffn_w_up, L0_ffn_w_down)
    return x

_drawn_inputs = setup_inputs


def setup_inputs(seed=0):
    import zlib

    import numpy as np

    out = dict(_drawn_inputs(seed))
    spreads = {}
    factors = {'L0_xattn_igate_bias': 64.0}
    for name, (base, spread) in spreads.items():
        noise = np.random.default_rng([zlib.crc32(name.encode()), seed]).standard_normal(out[name].shape)
        drawn = base * np.exp(spread * noise) if base else spread * noise
        out[name] = jnp.asarray(drawn.astype(out[name].dtype))
    for name, factor in factors.items():
        out[name] = (out[name] * factor).astype(out[name].dtype)
    return out
```

```python
from contextlib import ExitStack

import concourse.bass as bass
from concourse import mybir

ALU = mybir.AluOpType
ACT = mybir.ActivationFunctionType
F32 = mybir.dt.float32
BF16 = mybir.dt.bfloat16
I32 = mybir.dt.int32
U32 = mybir.dt.uint32
AX_X = mybir.AxisListType.X

P = 128
NEG = -1.0e30
LN_EPS = 1e-5
NORM_EPS = 1e-6


def build(nc, x, ctx_in, ik, ib, fk, fb, w_router, w_gate, w_up, w_down, consts, out):
    B, S, D = x.shape
    NH = ik.shape[1]
    HD = D // NH
    H1 = HD + 1
    CH = S // P
    NT = B * CH
    G = D // P
    HG = P // HD
    E = w_gate.shape[0]
    T = B * S
    C = -(-5 * T // (4 * E))
    SLOTS = E * C
    ROW = D + 4
    NSLOT = 16
    LAG = 5
    STEPS = NT + LAG + 1

    xbuf = nc.dram_tensor("xbuf", [SLOTS, ROW], F32).ap()
    x_t = x.rearrange("b (c p) d -> p (b c) d", p=P)
    ctx_t = ctx_in.rearrange("b (c p) d -> p (b c) d", p=P)
    out_rows = out.rearrange("b s d -> (b s) d")
    out_t = out.rearrange("b (c p) d -> p (b c) d", p=P)

    with ExitStack() as stack:
        def sb(name, shape, dt=F32):
            return stack.enter_context(nc.sbuf_tensor(name, shape, dt))

        def psum(name, shape, dt=F32):
            return stack.enter_context(nc.psum_tensor(name, shape, dt))

        def sem(name):
            return stack.enter_context(nc.semaphore(name))

        W = sb("W", [P, NSLOT, 3, G, D])
        Wflat = W[:].rearrange("p s m g d -> p s (m g d)")
        rowsX = sb("rowsX", [P, NT, ROW])
        ctxN = sb("ctxN", [P, NT, D])
        qkT = sb("qkT", [P, 2 * G, T])
        qT, kT = qkT[:, 0:G, :], qkT[:, G:2 * G, :]
        decay = sb("decay", [P, 3, NH * P])
        xn = sb("xn", [P, 2, D])
        st1 = sb("st1", [P, NT, 6])
        mv1 = sb("mv1", [P, NT, 2])
        ve = sb("ve", [P, 2, NH, H1])
        vp = sb("vp", [P, 2, NH, H1])
        carried = sb("carried", [P, NH, H1])
        hs = sb("hs", [P, 2, NH, H1])
        sq = sb("sq", [P, NH, HD])
        xt = sb("xt", [P, 2, D])
        xtT = sb("xtT", [P, 2, G, P])
        base = sb("base", [P, 2, D])
        state = sb("state", [P, 2, G, HG * H1])
        fresh = sb("fresh", [P, G * HG * H1])
        tok = sb("tok", [P, CH, P])
        chdec = sb("chdec", [P, B * G, 2])
        small = sb("small", [P, 8, NH])
        st2 = sb("st2", [P, 6])
        mv2 = sb("mv2", [P, 2])
        gsb = sb("gsb", [P, CH * 2 * B * NH])
        logits = sb("logits", [P, CH, E])
        lwork = sb("lwork", [P, 4, CH, E])
        hot = sb("hot", [P, B, CH, E], BF16)
        hotsum = sb("hotsum", [P, E], BF16)
        hotpart = sb("hotpart", [P, E], BF16)
        rsm = sb("rsm", [P, 8, CH])
        slot = sb("slot", [P, NT], U32)
        wgq = sb("wgq", [P, G, 2, NH])
        wgk = sb("wgk", [P, G, 2, NH])
        wgv = sb("wgv", [P, G, 2, NH])
        wr = sb("wr", [P, G, E])
        bias = sb("bias", [2 * B * NH, 1])
        NC = consts.shape[1]
        cst = sb("cst", [P, NC])
        cstb = sb("cstb", [P, 2 * P], BF16)
        xinit = sb("xinit", [P, ROW])

        ident = cst[:, 0:P]
        o = P
        blockmask = cst[:, o:o + G * HG * H1]; o += G * HG * H1
        headrow = cst[:, o:o + P]; o += P
        bgmask = cst[:, o:o + B * G]; o += B * G
        rev = cst[:, o:o + E]; o += E
        tri_f = cst[:, o:o + 2 * P]; o += 2 * P
        neghalf = cst[:, o:o + NH]; o += NH
        assert o == NC
        tri, ones = cstb[:, 0:P], cstb[:, P:2 * P]

        R = B * NH
        gates_sb, logf, cumf, a_row, m_row, one_row = (
            Wflat[:, NSLOT - 2 + i // 3, (i % 3) * S:(i % 3 + 1) * S] for i in range(6))
        args = sb("args", [P, S])
        m_seq = Wflat[:, NSLOT - 5:NSLOT - 2, :].rearrange("p s n -> p (s n)")[:, 0:CH * NH * P].rearrange(
            "p (c n) -> p c n", c=CH)
        LATE = 5

        pool_f = qkT[:].rearrange("p a t -> p (a t)")
        NR = 8
        f = [0]

        def cut(n):
            f[0] += n
            return pool_f[:, f[0] - n:f[0]]

        erow = cut(NR * ROW).rearrange("p (e r) -> p e r", e=NR)
        ext = cut(2 * D).rearrange("p (e r) -> p e r", e=2)
        ebase = cut(4 * D).rearrange("p (e r) -> p e r", e=4)
        eout = cut(4 * D).rearrange("p (e r) -> p e r", e=4)
        extT = cut(2 * G * C).rearrange("p (e g c) -> p e g c", e=2, g=G)
        esil = cut(2 * G * C).rearrange("p (e g c) -> p e g c", e=2, g=G)
        ehT = cut(2 * G * C).rearrange("p (e g c) -> p e g c", e=2, g=G)

        pq = psum("pq", [P, 4, 512])
        pown = psum("pown", [P, 512])
        pearly = psum("pearly", [P, 512])
        pstate = psum("pstate", [P, 512])
        pmisc = psum("pmisc", [P, 512])
        pgate = pown[:, 0:CH * 2 * B * NH].rearrange("p (c g b h) -> p c g b h", c=CH, g=2, b=B)
        own = pown[:, 0:NH * H1]
        early = pearly[:, 0:NH * H1]
        xtT_ps = pmisc[:, 0:G * P]
        log_ps = pmisc[:, 256:256 + E]
        cnt_ps = pmisc[:, 320:320 + CH * E]

        x_in = [sem(f"x_in{b}") for b in range(B)]
        c_in = [sem(f"c_in{b}") for b in range(B)]
        cst_in, par_in, par_in2 = sem("cst_in"), sem("par_in"), sem("par_in2")
        w_in = [sem(f"w_in{s}") for s in range(NSLOT)]
        init_set, init_out = sem("init_set"), sem("init_out")
        wk_sum, cstb_set, ones_set = sem("wk_sum"), sem("cstb_set"), sem("ones_set")
        ln1_ready, xn_ready, tr1_ready, qk_copied = sem("ln1_ready"), sem("xn_ready"), sem("tr1_ready"), sem("qk_copied")
        rstd1_ready = sem("rstd1_ready")
        gates_done, gates_copied, gatesT_done, gatesT_copied = (
            sem("gates_done"), sem("gates_copied"), sem("gatesT_done"), sem("gatesT_copied"))
        softplus_ready, gate_step, args_ready, exps_ready = (
            sem("softplus_ready"), sem("gate_step"), sem("args_ready"), sem("exps_ready"))
        act_gate = sem("act_gate")
        m_ready, m_in = sem("m_ready"), sem("m_in")
        tokT_done, tok_ready, chsel_ready, chdec_done, chdec_ready = (
            sem("tokT_done"), sem("tok_ready"), sem("chsel_ready"), sem("chdec_done"), sem("chdec_ready"))
        mb_raw, mb_ready = sem("mb_raw"), sem("mb_ready")
        ve_ready, vp_ready = sem("ve_ready"), sem("vp_ready")
        scores_done, exp_done, c_ready = sem("scores_done"), sem("exp_done"), sem("c_ready")
        own_done, early_done, state_done, state_ready = (
            sem("own_done"), sem("early_done"), sem("state_done"), sem("state_ready"))
        fresh_ready, carried_ready, hs_ready = sem("fresh_ready"), sem("carried_ready"), sem("hs_ready")
        sq_ready, z_ready, r_ready = sem("sq_ready"), sem("z_ready"), sem("r_ready")
        norm_step, var_ready, rstd_ready, xt_ready = (
            sem("norm_step"), sem("var_ready"), sem("rstd_ready"), sem("xt_ready"))
        base_ready = sem("base_ready")
        base_out = [sem(f"base_out{i}") for i in range(2)]
        xtT_done, xtT_ready, log_done, log_ready = sem("xtT_done"), sem("xtT_ready"), sem("log_done"), sem("log_ready")
        route_step, lexp_in, lexp_ready, hot_ready, cnt_done, slot_ready = (
            sem("route_step"), sem("lexp_in"), sem("lexp_ready"), sem("hot_ready"), sem("cnt_done"), sem("slot_ready"))
        cnt_read = sem("cnt_read")
        rows_out = sem("rows_out")
        erow_in = [sem(f"erow_in{i}") for i in range(2)]
        e_xt, e_xtT_done, e_xtT, e_base = sem("e_xt"), sem("e_xtT_done"), sem("e_xtT"), sem("e_base")
        e_gu, e_sil, e_h, e_y, e_out = sem("e_gu"), sem("e_sil"), sem("e_h"), sem("e_y"), sem("e_out")
        e_stored = [sem(f"e_stored{i}") for i in range(4)]
        idset = sem("idset")

        block = stack.enter_context(nc.Block())

        def chunk(n):
            return slice(n * P, (n + 1) * P)

        def n_state(n):
            return (n // CH) * (CH - 1) + min(n % CH + 1, CH - 1)

        @block.sync
        def _(sp):
            for b in range(B):
                sp.dma_start(rowsX[:, b * CH:(b + 1) * CH, 0:D], x_t[:, b * CH:(b + 1) * CH, :]).then_inc(x_in[b], 16)
                if b == 0:
                    sp.dma_start(cst[:], consts).then_inc(cst_in, 16)
                sp.dma_start(ctxN[:, b * CH:(b + 1) * CH, :], ctx_t[:, b * CH:(b + 1) * CH, :]).then_inc(c_in[b], 16)
                if b == 0:
                    with nc.allow_non_contiguous_dma(reason="small parameters"):
                        for i, kern in enumerate((ik, fk)):
                            for j, dst in enumerate((wgq, wgk, wgv)):
                                sp.dma_start(dst[:, :, i, :], kern[j * D:(j + 1) * D, :].rearrange(
                                    "(g p) h -> p g h", p=P)).then_inc(par_in, 16)
                        sp.dma_start(wr[:], w_router.rearrange("(g p) e -> p g e", p=P)).then_inc(par_in2, 16)
                        for i, bb in enumerate((ib, fb)):
                            for r in range(B):
                                lo = (i * B + r) * NH
                                sp.dma_start(bias[lo:lo + NH, :], bb.rearrange("(h a) -> h a", a=1)).then_inc(par_in2, 16)
            sp.wait_ge(init_set, 2)
            k = SLOTS // P
            sp.dma_start(xbuf.rearrange("(p k) r -> p k r", k=k),
                         xinit[:].unsqueeze(1).broadcast_to([P, k, ROW])).then_inc(init_out, 16)

            def load_expert(e):
                s = e % NSLOT
                for m, w in enumerate((w_gate, w_up, w_down)):
                    sp.dma_start(W[:, s, m, :, :], w[e].rearrange("(p g) f -> p g f", g=G)).then_inc(w_in[s], 16)

            for e in range(NSLOT - LATE):
                load_expert(e)
            sp.wait_ge(m_ready, 1)
            for b in range(B):
                for c in range(CH):
                    sp.dma_start(m_seq[32 * b:32 * b + 1, c, :].rearrange("p (h i) -> p h i", h=NH),
                                 one_row[b * NH:(b + 1) * NH, chunk(c)]).then_inc(m_in, 16)

            def store_base(n):
                sp.wait_ge(base_ready, n + 1)
                sp.dma_start(out_t[:, n, :], base[:, n % 2, :]).then_inc(base_out[n % 2], 16)

            for n in range(NT):
                store_base(n)
            sp.wait_ge(mb_raw, NT)
            sp.wait_ge(exps_ready, 1)
            for e in range(NSLOT - LATE, NSLOT):
                load_expert(e)

            def load_rows(q):
                sp.dma_start(erow[0:C, 4 * (q % 2):4 * (q % 2) + 4, :],
                             xbuf[4 * q * C:4 * (q + 1) * C, :].rearrange("(e c) r -> c e r", c=C)
                             ).then_inc(erow_in[q % 2], 16)

            sp.wait_ge(rows_out, 16 * NT)
            load_rows(0)
            load_rows(1)
            for e in range(E):
                if e % 4 == 3 and e // 4 + 2 < E // 4:
                    for i in range(4):
                        sp.wait_ge(e_stored[i], 16 * (e // 4 + 1))
                    load_rows(e // 4 + 2)
                if e + NSLOT < E:
                    sp.wait_ge(e_y, e + 1)
                    load_expert(e + NSLOT)
            for i in range(4):
                sp.wait_ge(e_stored[i], 16 * (E // 4))

        @block.gpsimd
        def _(pool):
            nc.gpsimd.memset(xinit[:], 0.0).then_inc(init_set, 1)
            pool.wait_ge(init_set, 1)
            nc.gpsimd.iota(xinit[:, D + 3:D + 4].bitcast(I32), pattern=[[0, 1]], base=T,
                           channel_multiplier=0).then_inc(init_set, 1)
            nc.gpsimd.iota(rowsX[:, :, D + 3].bitcast(I32), pattern=[[P, NT]], base=0,
                           channel_multiplier=1).then_inc(idset, 1)
            nc.gpsimd.memset(ve[:, :, :, HD:H1], 1.0).then_inc(ones_set, 1)
            nc.gpsimd.memset(Wflat[0:R, NSLOT - 1, 2 * S:3 * S], 1.0).then_inc(ones_set, 1)
            pool.wait_ge(cst_in, 16)
            for b in range(B):
                pool.wait_ge(ln1_ready, b + 1)
                v = mv1[:, b * CH:(b + 1) * CH, 1]
                nc.gpsimd.tensor_tensor(v, v, neghalf[:, 0:CH], ALU.pow).then_inc(rstd1_ready, 1)

            def broadcast_m(n):
                b, c = divmod(n, CH)
                pool.wait_ge(m_in, 16 * NT)
                if n >= 3:
                    pool.wait_ge(own_done, n - 2)
                for signal, count in ((mb_ready, n), (ve_ready, n - 1), (vp_ready, n_state(n - 2) if n >= 2 else 0),
                                      (r_ready, n - 2), (rstd_ready, n - 3), (base_ready, n - 4)):
                    if count > 0:
                        pool.wait_ge(signal, count)
                if n >= 2 and (n - 2 - LAG) // CH > 0:
                    pool.wait_ge(rows_out, 16 * CH * ((n - 2 - LAG) // CH))
                nc.gpsimd.partition_broadcast(decay[:, n % 3, :], m_seq[32 * b:32 * b + 1, c, :],
                                              channels=P).then_inc(mb_raw, 1)
                pool.wait_ge(mb_raw, n + 1)
                v = decay[:, n % 3, :].rearrange("p (h i) -> p h i", i=P)
                nc.gpsimd.affine_select(out=v, in_=v, compare_op=ALU.is_ge, fill=NEG, base=0,
                                        pattern=[[0, NH], [1, P]], channel_multiplier=-1).then_inc(mb_ready, 1)

            def values(n):
                b, c = divmod(n, CH)
                if n >= 2:
                    pool.wait_ge(own_done, n - 1)
                nc.gpsimd.tensor_copy(ve[:, n % 2, :, 0:HD],
                                      ctxN[:, n, :].rearrange("p (h d) -> p h d", h=NH)).then_inc(ve_ready, 1)
                if c < CH - 1:
                    pool.wait_ge(ve_ready, n + 1)
                    pool.wait_ge(tok_ready, 1)
                    if n_state(n) > 2:
                        pool.wait_ge(state_done, n_state(n) - 2)
                    w = tok[:, c, b * NH:(b + 1) * NH].unsqueeze(2).broadcast_to([P, NH, H1])
                    nc.gpsimd.tensor_tensor(vp[:, n_state(n) % 2], ve[:, n % 2], w, ALU.mult).then_inc(vp_ready, 1)

            pool.wait_ge(ones_set, 2)
            pool.wait_ge(c_in[0], 16)
            broadcast_m(0)
            for s in range(STEPS + 1):
                if s + 1 < NT:
                    broadcast_m(s + 1)
                if s >= LAG + CH and (s - LAG) % CH == 0 and (s - LAG) // CH <= B:
                    b = (s - LAG) // CH - 1
                    pool.wait_ge(slot_ready, b + 1)
                    if b == 0:
                        pool.wait_ge(init_out, 16)
                        pool.wait_ge(idset, 1)
                    for n in range(b * CH, (b + 1) * CH):
                        nc.gpsimd.indirect_dma_start(
                            out=xbuf, out_offset=bass.IndirectOffsetOnAxis(ap=slot[:, n:n + 1], axis=0),
                            in_=rowsX[:, n, :], in_offset=None, bounds_check=SLOTS - 1,
                            oob_is_err=False).then_inc(rows_out, 16)
                if s < NT:
                    if s % CH == 0:
                        pool.wait_ge(c_in[s // CH], 16)
                    values(s)
                n = s - 1
                if 0 <= n < NT:
                    pool.wait_ge(z_ready, n + 1)
                    if n >= 2:
                        pool.wait_ge(norm_step, n - 1)
                    nc.gpsimd.tensor_tensor(small[:, 4 + n % 2, :], small[:, 2 + n % 2, :], neghalf,
                                            ALU.pow).then_inc(r_ready, 1)
                n = s - 2
                if 0 <= n < NT:
                    pool.wait_ge(var_ready, n + 1)
                    v = rowsX[:, n, D + 1:D + 2]
                    nc.gpsimd.tensor_tensor(v, v, neghalf[:, 0:1], ALU.pow).then_inc(rstd_ready, 1)
                n = s - 3
                if 0 <= n < NT:
                    pool.wait_ge(xt_ready, n + 1)
                    if n >= 2:
                        pool.wait_ge(base_out[n % 2], 16 * (n // 2))
                    nc.gpsimd.tensor_tensor(base[:, n % 2, :], rowsX[:, n, 0:D], xt[:, n % 2, :],
                                            ALU.add).then_inc(base_ready, 1)
            for i in range(2):
                pool.wait_ge(base_out[i], 16 * NT // 2)
            for e in range(E + 2):
                if e < E:
                    pool.wait_ge(e_xt, e + 1)
                    if e >= 4:
                        pool.wait_ge(e_out, e - 3)
                    nc.gpsimd.tensor_tensor(ebase[0:C, e % 4, :], erow[0:C, e % NR, 0:D], ext[0:C, e % 2, :],
                                            ALU.add).then_inc(e_base, 1)
                d = e - 2
                if d >= 0:
                    pool.wait_ge(e_out, d + 1)
                    nc.gpsimd.indirect_dma_start(
                        out=out_rows, out_offset=bass.IndirectOffsetOnAxis(
                            ap=erow[0:C, d % NR, D + 3:D + 4].bitcast(U32), axis=0),
                        in_=eout[0:C, d % 4, :], in_offset=None, bounds_check=T - 1,
                        oob_is_err=False).then_inc(e_stored[d % 4], 16)

        @block.scalar
        def _(act):
            for n in range(NT):
                act.wait_ge(tr1_ready, n + 1)
                nc.scalar.copy(qkT[:, :, chunk(n)],
                               pq[:, n % 4, :].rearrange("p (a t) -> p a t", t=P)).then_inc(qk_copied, 1)
            act.wait_ge(gatesT_copied, 1)
            nc.scalar.activation(logf[0:R, :], gates_sb[R:2 * R, :], ACT.Abs).then_inc(act_gate, 1)
            act.wait_ge(act_gate, 1)
            nc.scalar.activation(logf[0:R, :], logf[0:R, :], ACT.Exp, scale=-1.0).then_inc(act_gate, 1)
            act.wait_ge(act_gate, 2)
            nc.scalar.activation(logf[0:R, :], logf[0:R, :], ACT.Ln, bias=1.0).then_inc(softplus_ready, 1)
            act.wait_ge(args_ready, 1)
            nc.scalar.activation(args[0:3 * R, :], args[0:3 * R, :], ACT.Exp).then_inc(exps_ready, 1)
            act.wait_ge(tokT_done, 1)
            nc.scalar.copy(tok[:], pstate[:].rearrange("p (c r) -> p c r", c=CH)).then_inc(tok_ready, 1)
            act.wait_ge(tok_ready, 1)
            for s in range(STEPS + 1):
                n = s
                if n < NT:
                    b, c = divmod(n, CH)
                    act.wait_ge(mb_ready, n + 1)
                    for h in range(NH):
                        v = decay[:, n % 3, h * P:(h + 1) * P]
                        last = nc.scalar.activation(v, v, ACT.Exp,
                                                    bias=tok[:, c, 3 * R + b * NH + h:3 * R + b * NH + h + 1])
                    last.then_inc(exp_done, 1)
                n = s - 4
                if 0 <= n < NT:
                    act.wait_ge(log_done, n + 1)
                    if n >= CH and n % CH == 0:
                        act.wait_ge(hot_ready, n // CH)
                    nc.scalar.copy(logits[:, n % CH, :], log_ps).then_inc(log_ready, 1)
                n = s - 1
                if 0 <= n < NT:
                    act.wait_ge(hs_ready, n + 1)
                    if n >= 1:
                        act.wait_ge(z_ready, n)
                    nc.scalar.activation(sq[:], hs[:, n % 2, :, 0:HD], ACT.Square,
                                         scale=float(HD) ** -0.5).then_inc(sq_ready, 1)
                n = s - 3
                if 0 <= n < NT:
                    act.wait_ge(xtT_done, n + 1)
                    if n >= 2:
                        act.wait_ge(log_done, n - 1)
                    nc.scalar.copy(xtT[:, n % 2], xtT_ps.rearrange("p (g t) -> p g t", g=G)).then_inc(xtT_ready, 1)
                if s >= 4 and (s - 4) % CH == CH - 1:
                    b = (s - 4) // CH
                    act.wait_ge(lexp_in, b + 1)
                    nc.scalar.activation(lwork[:, 1], lwork[:, 0], ACT.Exp).then_inc(lexp_ready, 1)
            for e in range(E):
                act.wait_ge(e_gu, e + 1)
                if e >= 2:
                    act.wait_ge(e_h, e - 1)
                nc.scalar.activation(esil[:, e % 2], pq[:, e % 2, 0:G * C].rearrange("p (g c) -> p g c", g=G),
                                     ACT.Silu).then_inc(e_sil, 1)

        @block.tensor
        def _(pe):
            def gates(n):
                b, c = divmod(n, CH)
                pe.wait_ge(qk_copied, n + 1)
                for i in range(2 * G):
                    w = (wgq if i < G else wgk)[:, i % G]
                    last = nc.tensor.matmul(pgate[:, c, :, b, :], qkT[:, i, chunk(n)], w,
                                            start=(i == 0), stop=(i == 2 * G - 1))
                last.then_inc(gates_done, 1)

            pe.wait_ge(cst_in, 16)
            for n in range(NT):
                if n % CH == 0:
                    pe.wait_ge(c_in[n // CH], 16)
                pe.wait_ge(xn_ready, n + 1)
                if n >= 4:
                    pe.wait_ge(qk_copied, n - 3)
                for i in range(2 * G):
                    src = xn[:, n % 2, i * P:(i + 1) * P] if i < G else ctxN[:, n, (i - G) * P:(i - G + 1) * P]
                    last = nc.tensor.transpose(pq[:, n % 4, i * P:(i + 1) * P], src, ident)
                last.then_inc(tr1_ready, 1)
                if n == 1:
                    pe.wait_ge(wk_sum, 1)
                if n >= 1:
                    gates(n - 1)
            gates(NT - 1)
            pe.wait_ge(gates_copied, 1)
            for c in range(CH):
                last = nc.tensor.transpose(pearly[0:2 * R, chunk(c)], gsb[:, c * 2 * R:(c + 1) * 2 * R], ident)
            last.then_inc(gatesT_done, 1)
            pe.wait_ge(exps_ready, 1)
            pe.wait_ge(args_ready, 2)
            for c in range(CH):
                last = nc.tensor.transpose(pstate[:, chunk(c)], args[:, chunk(c)], ident)
            last.then_inc(tokT_done, 1)
            pe.wait_ge(chsel_ready, 1)
            nc.tensor.matmul(pmisc[:, 0:2 * B * G], headrow[R:2 * R, :], gsb[R:2 * R, 0:2 * B * G],
                             start=True, stop=True).then_inc(chdec_done, 1)

            def scores(n):
                if n >= 1:
                    pe.wait_ge(c_ready, n)
                else:
                    pe.wait_ge(qk_copied, NT)
                for g in range(G):
                    for h in range(HG):
                        r = slice(h * HD, (h + 1) * HD)
                        last = nc.tensor.matmul(pq[:, h, g * P:(g + 1) * P], kT[r, g, chunk(n)], qT[r, g, chunk(n)],
                                                start=True, stop=True)
                last.then_inc(scores_done, 1)

            def outputs(n):
                c = n % CH
                if c > 0:
                    pe.wait_ge(state_ready, n_state(n - 1))
                    if n_state(n - 1) > 1:
                        pe.wait_ge(carried_ready, n_state(n - 1) - 1)
                    for g in range(G):
                        w = HG * H1
                        last = nc.tensor.matmul(early[:, g * w:(g + 1) * w], qT[:, g, chunk(n)],
                                                state[:, n_state(n - 1) % 2, g, :], start=True, stop=True)
                    last.then_inc(early_done, 1)
                pe.wait_ge(c_ready, n + 1)
                pe.wait_ge(ve_ready, n + 1)
                if n == 0:
                    pe.wait_ge(gates_copied, 1)
                else:
                    pe.wait_ge(hs_ready, n)
                for h in range(NH):
                    last = nc.tensor.matmul(own[:, h * H1:(h + 1) * H1], decay[:, n % 3, h * P:(h + 1) * P],
                                            ve[:, n % 2, h, :], start=True, stop=True)
                last.then_inc(own_done, 1)

            def state_sum(n):
                k = n_state(n)
                pe.wait_ge(vp_ready, k)
                if k > 1:
                    pe.wait_ge(fresh_ready, k - 1)
                else:
                    pe.wait_ge(tok_ready, 1)
                w = HG * H1
                for g in range(G):
                    last = nc.tensor.matmul(pstate[:, g * w:(g + 1) * w], ctxN[:, n, g * P:(g + 1) * P],
                                            vp[:, k % 2, g * HG:(g + 1) * HG, :].rearrange("p h d -> p (h d)"),
                                            start=True, stop=True)
                last.then_inc(state_done, 1)

            for s in range(STEPS + 1):
                if s < NT:
                    scores(s)
                n = s - 4
                if 0 <= n < NT:
                    pe.wait_ge(xtT_ready, n + 1)
                    if n == 0:
                        pe.wait_ge(par_in2, 16 * (1 + 2 * B))
                    for g in range(G):
                        last = nc.tensor.matmul(log_ps, xtT[:, n % 2, g, :], wr[:, g, :], start=(g == 0),
                                                stop=(g == G - 1))
                    last.then_inc(log_done, 1)
                if s >= LAG + CH - 1 and (s - LAG) % CH == CH - 1 and (s - LAG) // CH < B:
                    b = (s - LAG) // CH
                    pe.wait_ge(hot_ready, b + 1)
                    pe.wait_ge(log_ready, min(NT, s - 4 + 1))
                    for t in range(CH):
                        o_ = cnt_ps[:, t * E:(t + 1) * E]
                        nc.tensor.matmul(o_, ones, hotsum[:], start=True, stop=False)
                        for u in range(t):
                            nc.tensor.matmul(o_, ones, hot[:, b, u, :], start=False, stop=False)
                        last = nc.tensor.matmul(o_, tri, hot[:, b, t, :], start=False, stop=True)
                    last.then_inc(cnt_done, 1)
                n = s - 1
                if 0 <= n < NT:
                    outputs(n)
                if s < NT and s % CH < CH - 1:
                    state_sum(s)
                n = s - 3
                if 0 <= n < NT:
                    pe.wait_ge(xt_ready, n + 1)
                    if n >= 1:
                        pe.wait_ge(log_ready, n)
                    else:
                        pe.wait_ge(chdec_ready, 1)
                    k = (s - LAG) // CH + (1 if (s - LAG) % CH == CH - 1 else 0)
                    if s >= LAG and k >= 1:
                        pe.wait_ge(cnt_read, k)
                    for g in range(G):
                        last = nc.tensor.transpose(xtT_ps[:, g * P:(g + 1) * P], xt[:, n % 2, g * P:(g + 1) * P], ident)
                    last.then_inc(xtT_done, 1)

            def e_transpose(e):
                pe.wait_ge(e_xt, e + 1)
                if e >= 2:
                    pe.wait_ge(e_xtT, e - 1)
                bank = (pown, pearly)[e % 2]
                v = ext[0:C, e % 2, :].rearrange("c (p g) -> c g p", g=G)
                for g in range(G):
                    last = nc.tensor.transpose(bank[:, g * C:(g + 1) * C], v[:, g, :], ident[0:C, 0:C])
                last.then_inc(e_xtT_done, 1)

            def e_gate_up(e):
                s = e % NSLOT
                pe.wait_ge(w_in[s], 48 * (e // NSLOT + 1))
                pe.wait_ge(e_xtT, e + 1)
                if e >= 2:
                    pe.wait_ge(e_h, e - 1)
                for m in range(2):
                    for j in range(G):
                        o_ = pq[:, e % 2, (m * G + j) * C:(m * G + j + 1) * C]
                        for g in range(G):
                            w = W[:, s, m, g, :].rearrange("p (m j) -> p j m", j=G)[:, j, :]
                            last = nc.tensor.matmul(o_, w, extT[:, e % 2, g, :], start=(g == 0), stop=(g == G - 1))
                last.then_inc(e_gu, 1)

            def e_down(e):
                pe.wait_ge(e_h, e + 1)
                if e >= 2:
                    pe.wait_ge(e_out, e - 1)
                for j in range(G):
                    last = nc.tensor.matmul(pq[0:C, 2 + e % 2, 0:D], ehT[:, e % 2, j, :], W[:, e % NSLOT, 2, j, :],
                                            start=(j == 0), stop=(j == G - 1))
                last.then_inc(e_y, 1)

            e_transpose(0)
            for e in range(E):
                if e + 1 < E:
                    e_transpose(e + 1)
                e_gate_up(e)
                if e >= 1:
                    e_down(e - 1)
            e_down(E - 1)

        @block.vector
        def _(dve):
            V = nc.vector
            dve.wait_ge(par_in, 16 * 6)
            V.tensor_tensor(wgk[:], wgk[:], wgv[:], ALU.add).then_inc(wk_sum, 1)
            dve.wait_ge(cst_in, 16)
            V.tensor_copy(cstb[:], tri_f).then_inc(cstb_set, 1)
            V.memset(hotsum[:], 0.0).then_inc(cstb_set, 1)
            lnstep = [0]

            def xn_of(b):
                dve.wait_ge(rstd1_ready, b + 1)
                for n in range(b * CH, (b + 1) * CH):
                    if n >= 2:
                        dve.wait_ge(tr1_ready, n - 1)
                    V.tensor_scalar(xn[:, n % 2, :], rowsX[:, n, 0:D], mv1[:, n, 0:1], mv1[:, n, 1:2],
                                    ALU.subtract, ALU.mult).then_inc(xn_ready, 1)

            for b in range(B):
                dve.wait_ge(x_in[b], 16)
                for n in range(b * CH, (b + 1) * CH):
                    V.bn_stats(st1[:, n, :], rowsX[:, n, 0:D]).then_inc(gate_step, 1)
                for n in range(b * CH, (b + 1) * CH):
                    dve.wait_ge(gate_step, CH * 2 * b + b + n - b * CH + 1)
                    V.bn_aggr(mv1[:, n, :], st1[:, n, :]).then_inc(gate_step, 1)
                dve.wait_ge(gate_step, b * (2 * CH + 1) + 2 * CH)
                v = mv1[:, b * CH:(b + 1) * CH, 1]
                V.tensor_scalar(v, v, LN_EPS, None, ALU.add).then_inc(ln1_ready, 1)
                V.engine_nop().then_inc(gate_step, 1)
                if b >= 1:
                    xn_of(b - 1)
            xn_of(B - 1)
            gs = [B * (2 * CH + 1)]

            def step(ins):
                gs[0] += 1
                ins.then_inc(gate_step, 1)
                dve.wait_ge(gate_step, gs[0])

            dve.wait_ge(gates_done, NT)
            V.tensor_copy(gsb[:], pown[:, 0:CH * 2 * R]).then_inc(gates_copied, 1)
            dve.wait_ge(gatesT_done, 1)
            dve.wait_ge(par_in2, 16 * (1 + 2 * B))
            V.tensor_scalar(gates_sb[0:2 * R, :], pearly[0:2 * R, :], bias[:, 0:1], None,
                            ALU.add).then_inc(gatesT_copied, 1)
            dve.wait_ge(gatesT_copied, 1)
            step(V.tensor_scalar(cumf[0:R, :], gates_sb[R:2 * R, :], 0.0, None, ALU.min))
            dve.wait_ge(softplus_ready, 1)
            step(V.tensor_tensor(logf[0:R, :], cumf[0:R, :], logf[0:R, :], ALU.subtract))
            dve.wait_ge(ones_set, 2)
            step(V.tensor_tensor_scan(cumf[0:R, :], one_row[0:R, :], logf[0:R, :], 0.0, ALU.mult, ALU.add))
            step(V.tensor_tensor(a_row[0:R, :], gates_sb[0:R, :], cumf[0:R, :], ALU.subtract))
            step(V.tensor_tensor_scan(m_row[0:R, :], a_row[0:R, :], a_row[0:R, :], -3.0e38, ALU.max, ALU.max))
            V.tensor_scalar(one_row[0:R, :], m_row[0:R, :], -1.0, None, ALU.mult).then_inc(m_ready, 1)
            mr = m_row[0:R, :].rearrange("p (c i) -> p c i", c=CH)
            ar = a_row[0:R, :].rearrange("p (c i) -> p c i", c=CH)
            ends = mr[:, :, P - 1:P].broadcast_to([R, CH, P])
            A = args[:].rearrange("p (c i) -> p c i", c=CH)
            V.tensor_tensor(A[0:R], ar, ends, ALU.subtract)
            V.memset(A[R:2 * R, 0, :], 0.0)
            V.tensor_tensor(A[R:2 * R, 1:CH, :], mr[:, 0:CH - 1, P - 1:P].broadcast_to([R, CH - 1, P]), mr[:, 1:CH, :],
                            ALU.subtract)
            V.scalar_tensor_tensor(out=args[2 * R:3 * R, :], in0=cumf[0:R, :], scalar=-1.0, in1=m_row[0:R, :],
                                   op0=ALU.mult, op1=ALU.subtract).then_inc(args_ready, 1)
            V.tensor_copy(args[3 * R:4 * R, :], a_row[0:R, :]).then_inc(args_ready, 1)
            dve.wait_ge(exps_ready, 1)
            sel = gsb[R:2 * R, 0:2 * B * G].rearrange("p (g k) -> p g k", k=2)
            V.tensor_tensor(sel, bgmask[R:2 * R, :].unsqueeze(2).broadcast_to([R, B * G, 2]),
                            A[R:2 * R, 1:3, P - 1:P].rearrange("p a b -> p b a").broadcast_to([R, B * G, 2]),
                            ALU.mult).then_inc(chsel_ready, 1)
            dve.wait_ge(chdec_done, 1)
            V.tensor_copy(chdec[:], pmisc[:, 0:2 * B * G].rearrange("p (g k) -> p g k", k=2)).then_inc(chdec_ready, 1)
            dve.wait_ge(tok_ready, 1)
            dve.wait_ge(chdec_ready, 1)

            def decay_scores(n):
                dve.wait_ge(scores_done, n + 1)
                dve.wait_ge(exp_done, n + 1)
                for g in range(G):
                    v = decay[:, n % 3, g * HG * P:(g + 1) * HG * P].rearrange("p (h r) -> p h r", h=HG)
                    last = V.scalar_tensor_tensor(out=v, in0=pq[:, :, g * P:(g + 1) * P], scalar=float(HD) ** -0.5,
                                                  in1=v, op0=ALU.mult, op1=ALU.mult)
                last.then_inc(c_ready, 1)

            def combine(n):
                b, c = divmod(n, CH)
                if n >= 2:
                    dve.wait_ge(norm_step, n - 1)
                ow = own.rearrange("p (h d) -> p h d", h=NH)
                if c > 0:
                    w = tok[:, c, R + b * NH:R + (b + 1) * NH].unsqueeze(2).broadcast_to([P, NH, H1])
                    dve.wait_ge(early_done, n_state(n - 1))
                    V.tensor_tensor(carried[:], early.rearrange("p (h d) -> p h d", h=NH), w,
                                    ALU.mult).then_inc(carried_ready, 1)
                    dve.wait_ge(carried_ready, n_state(n - 1))
                    dve.wait_ge(own_done, n + 1)
                    V.tensor_tensor(hs[:, n % 2], ow, carried[:], ALU.add).then_inc(hs_ready, 1)
                else:
                    dve.wait_ge(own_done, n + 1)
                    V.tensor_copy(hs[:, n % 2], ow).then_inc(hs_ready, 1)
                dve.wait_ge(hs_ready, n + 1)
                total = hs[:, n % 2, :, HD]
                link(V.scalar_tensor_tensor(out=small[:, 0, :], in0=total, scalar=-1.0, in1=total, op0=ALU.mult,
                                            op1=ALU.max))
                link(V.tensor_tensor(small[:, 0, :], small[:, 0, :], tok[:, c, 2 * R + b * NH:2 * R + (b + 1) * NH],
                                     ALU.max))
                link(V.tensor_scalar(small[:, 0, :], small[:, 0, :], NORM_EPS, None, ALU.add))
                link(V.tensor_tensor(small[:, 0, :], small[:, 0, :], small[:, 0, :], ALU.mult))
                dve.wait_ge(sq_ready, n + 1)
                link(V.tensor_reduce(small[:, 1, :], sq[:], AX_X, ALU.add))
                if n >= 2:
                    dve.wait_ge(r_ready, n - 1)
                V.scalar_tensor_tensor(out=small[:, 2 + n % 2, :], in0=small[:, 0, :], scalar=1e-6,
                                       in1=small[:, 1, :], op0=ALU.mult, op1=ALU.add).then_inc(z_ready, 1)

            links = [0]

            def link(ins):
                links[0] += 1
                ins.then_inc(route_step, 1)
                dve.wait_ge(route_step, links[0])

            def update_state(n):
                k = n_state(n)
                b, c = divmod(n, CH)
                dve.wait_ge(state_done, k)
                if c == 0:
                    if k > 1:
                        dve.wait_ge(early_done, k - 1)
                    V.tensor_tensor(state[:, k % 2].rearrange("p g w -> p (g w)"), pstate[:, 0:G * HG * H1],
                                    blockmask, ALU.mult).then_inc(fresh_ready, 1)
                    dve.wait_ge(fresh_ready, k)
                    V.engine_nop().then_inc(state_ready, 1)
                    return
                V.tensor_tensor(fresh[:], pstate[:, 0:G * HG * H1], blockmask, ALU.mult).then_inc(fresh_ready, 1)
                dve.wait_ge(fresh_ready, k)
                dve.wait_ge(early_done, max(1, k - 2))
                w = HG * H1
                for g in range(G):
                    last = V.scalar_tensor_tensor(out=state[:, k % 2, g, :], in0=state[:, (k - 1) % 2, g, :],
                                                  scalar=chdec[:, b * G + g, c - 1:c], in1=fresh[:, g * w:(g + 1) * w],
                                                  op0=ALU.mult, op1=ALU.add)
                last.then_inc(state_ready, 1)

            def residual(n):
                dve.wait_ge(r_ready, n + 1)
                r = small[:, 4 + n % 2, :].unsqueeze(2).broadcast_to([P, NH, HD])
                hv = hs[:, n % 2, :, 0:HD]
                V.tensor_tensor(hv, hv, r, ALU.mult).then_inc(norm_step, 1)
                dve.wait_ge(norm_step, n + 1)
                xv = rowsX[:, n, 0:D]
                x3 = xv.rearrange("p (h d) -> p h d", h=NH)
                link(V.tensor_tensor(x3, x3, hv, ALU.add))
                link(V.bn_stats(st2[:], xv))
                link(V.bn_aggr(rowsX[:, n, D:D + 2], st2[:]))
                V.tensor_scalar(rowsX[:, n, D + 1:D + 2], rowsX[:, n, D + 1:D + 2], LN_EPS, None,
                                ALU.add).then_inc(var_ready, 1)

            def norm_x1(n):
                dve.wait_ge(rstd_ready, n + 1)
                if n >= 2:
                    dve.wait_ge(xtT_done, n - 1)
                    dve.wait_ge(base_ready, n - 1)
                V.tensor_scalar(xt[:, n % 2, :], rowsX[:, n, 0:D], rowsX[:, n, D:D + 1], rowsX[:, n, D + 1:D + 2],
                                ALU.subtract, ALU.mult).then_inc(xt_ready, 1)

            def choose(b):
                dve.wait_ge(log_ready, (b + 1) * CH)
                mx, g3, fm = rsm[:, 0, :], rsm[:, 1, :], rsm[:, 2, :]

                def wide(v):
                    return v.unsqueeze(2).broadcast_to([P, CH, E])
                link(V.tensor_reduce(mx, logits[:], AX_X, ALU.max))
                V.tensor_tensor(lwork[:, 0], logits[:], wide(mx), ALU.subtract).then_inc(lexp_in, 1)
                dve.wait_ge(lexp_in, b + 1)
                link(V.scalar_tensor_tensor(out=lwork[:, 2], in0=lwork[:, 0], scalar=0.0,
                                            in1=rev.unsqueeze(1).broadcast_to([P, CH, E]), op0=ALU.is_ge, op1=ALU.mult))
                link(V.tensor_reduce(fm, lwork[:, 2], AX_X, ALU.max))
                link(V.tensor_tensor(hot[:, b], lwork[:, 2], wide(fm), ALU.is_equal))
                V.engine_nop().then_inc(hot_ready, 1)
                dve.wait_ge(lexp_ready, b + 1)
                link(V.tensor_reduce(g3, lwork[:, 1], AX_X, ALU.add))
                link(V.reciprocal(rowsX[:, b * CH:(b + 1) * CH, D + 2], g3))

            def place(b):
                fm, pos, over, sl = (rsm[:, i, :] for i in range(2, 6))
                dve.wait_ge(cnt_done, b + 1)
                V.tensor_tensor(lwork[:, 3], cnt_ps.rearrange("p (t e) -> p t e", t=CH), hot[:, b],
                                ALU.mult).then_inc(cnt_read, 1)
                dve.wait_ge(cnt_read, b + 1)
                link(V.tensor_reduce(pos, lwork[:, 3], AX_X, ALU.add))
                link(V.tensor_scalar(over, pos, float(C), float(2 * SLOTS), ALU.is_ge, ALU.mult))
                link(V.scalar_tensor_tensor(out=sl, in0=fm, scalar=-float(C), in1=pos, op0=ALU.mult, op1=ALU.add))
                link(V.tensor_tensor(sl, sl, over, ALU.add))
                V.tensor_scalar(slot[:, b * CH:(b + 1) * CH], sl, float(E * C), None, ALU.add).then_inc(slot_ready, 1)
                if b + 1 < B:
                    with nc.allow_low_precision(reason="counts up to 16 are exact in bfloat16"):
                        link(V.tensor_reduce(hotpart[:], hot[:, b].rearrange("p t e -> p e t"), AX_X, ALU.add))
                    link(V.tensor_tensor(hotsum[:], hotsum[:], hotpart[:], ALU.add))

            dve.wait_ge(cstb_set, 2)
            for s in range(STEPS + 1):
                if 0 <= s - 3 < NT:
                    norm_x1(s - 3)
                if s < NT:
                    decay_scores(s)
                if 0 <= s - 1 < NT:
                    combine(s - 1)
                if s < NT and s % CH < CH - 1:
                    update_state(s)
                if 0 <= s - 2 < NT:
                    residual(s - 2)
                if s >= LAG + CH - 1 and (s - LAG) % CH == CH - 1 and (s - LAG) // CH < B:
                    place((s - LAG) // CH)
                if s >= 4 and (s - 4) % CH == CH - 1 and (s - 4) // CH < B:
                    choose((s - 4) // CH)

            def e_norm(e):
                if e % 4 == 0:
                    dve.wait_ge(erow_in[e // 4 % 2], 16 * (e // 8 + 1))
                if e >= 2:
                    dve.wait_ge(e_xtT_done, e - 1)
                    dve.wait_ge(e_base, e - 1)
                r = erow[0:C, e % NR, :]
                V.tensor_scalar(ext[0:C, e % 2, :], r[:, 0:D], r[:, D:D + 1], r[:, D + 1:D + 2],
                                ALU.subtract, ALU.mult).then_inc(e_xt, 1)

            def e_evac(e):
                dve.wait_ge(e_xtT_done, e + 1)
                if e >= 2:
                    dve.wait_ge(e_gu, e - 1)
                V.tensor_copy(extT[:, e % 2], (pown, pearly)[e % 2][:, 0:G * C].rearrange(
                    "p (g c) -> p g c", g=G)).then_inc(e_xtT, 1)

            def e_mul(e):
                dve.wait_ge(e_sil, e + 1)
                if e >= 2:
                    dve.wait_ge(e_y, e - 1)
                V.tensor_tensor(ehT[:, e % 2], pq[:, e % 2, G * C:2 * G * C].rearrange("p (g c) -> p g c", g=G),
                                esil[:, e % 2], ALU.mult).then_inc(e_h, 1)

            def e_combine(e):
                dve.wait_ge(e_y, e + 1)
                dve.wait_ge(e_base, e + 1)
                if e >= 4:
                    dve.wait_ge(e_stored[e % 4], 16 * (e // 4))
                V.scalar_tensor_tensor(out=eout[0:C, e % 4, :], in0=pq[0:C, 2 + e % 2, 0:D],
                                       scalar=erow[0:C, e % NR, D + 2:D + 3], in1=ebase[0:C, e % 4, :],
                                       op0=ALU.mult, op1=ALU.add).then_inc(e_out, 1)

            e_norm(0)
            e_evac(0)
            e_norm(1)
            for e in range(E):
                if e + 1 < E:
                    e_evac(e + 1)
                if e + 2 < E:
                    e_norm(e + 2)
                e_mul(e)
                if e >= 1:
                    e_combine(e - 1)
            e_combine(E - 1)


_INS = ['x', 'ctx_1024', 'L0_xattn_igate_kernel', 'L0_xattn_igate_bias', 'L0_xattn_fgate_kernel',
        'L0_xattn_fgate_bias', 'L0_ffn_w_router', 'L0_ffn_w_gate', 'L0_ffn_w_up', 'L0_ffn_w_down']


def shape_constants(B, D, NH, E):
    import numpy as np
    HD = D // NH
    G, HG, H1 = D // P, P // HD, HD + 1
    R = B * NH
    p = np.arange(P)
    ident = np.eye(P)
    head = np.repeat(np.arange(HG), H1)
    blockmask = np.tile((p[:, None] // HD == head[None, :]) * HD ** -0.5, (1, G))
    r = p - R
    headrow = (r[:, None] % HG == p[None, :] // HD) * 1.0
    bgmask = (r[:, None] // HG == np.arange(B * G)[None, :]) * 1.0
    rev = np.tile(E - np.arange(E), (P, 1))
    before = (p[:, None] < p[None, :]) * 1.0
    return np.concatenate([ident, blockmask, headrow, bgmask, rev, before, np.ones((P, P)),
                           np.full((P, NH), -0.5)], axis=1).astype(np.float32)


def kernel(**inputs):
    import numpy as _np
    import concourse.bacc as _bacc
    from concourse import mybir as _mybir
    from concourse.bass_utils import run_bass_kernel_spmd as _run

    nc = _bacc.Bacc("TRN2", target_bir_lowering=False, num_devices=1)
    arrays, args = {}, []
    for name in _INS:
        a = _np.ascontiguousarray(inputs[name])
        arrays[f"in_{name}_dram"] = a
        args.append(nc.dram_tensor(f"in_{name}_dram", a.shape, _mybir.dt.from_np(a.dtype), kind="ExternalInput").ap())
    b, s, d = inputs['x'].shape
    c = shape_constants(b, d, inputs['L0_xattn_igate_kernel'].shape[1], inputs['L0_ffn_w_gate'].shape[0])
    arrays["in_consts_dram"] = c
    args.append(nc.dram_tensor("in_consts_dram", c.shape, _mybir.dt.from_np(c.dtype), kind="ExternalInput").ap())
    args.append(nc.dram_tensor("out_0_dram", (b, s, d), _mybir.dt.float32, kind="ExternalOutput").ap())
    build(nc, *args)
    r = _run(nc, [arrays], core_ids=[0])
    return r.results[0]["out_0_dram"]
```

```python
from contextlib import ExitStack

import concourse.bass as bass
from concourse import mybir

ALU = mybir.AluOpType
ACT = mybir.ActivationFunctionType
F32 = mybir.dt.float32
BF16 = mybir.dt.bfloat16
I32 = mybir.dt.int32
U32 = mybir.dt.uint32
AX_X = mybir.AxisListType.X

P = 128
NEG = -1.0e30
LN_EPS = 1e-5
NORM_EPS = 1e-6


def build(nc, x, ctx_in, ik, ib, fk, fb, w_router, w_gate, w_up, w_down, consts, out):
    B, S, D = x.shape
    NH = ik.shape[1]
    HD = D // NH
    H1 = HD + 1
    CH = S // P
    NT = B * CH
    G = D // P
    HG = P // HD
    E = w_gate.shape[0]
    T = B * S
    C = -(-5 * T // (4 * E))
    SLOTS = E * C
    ROW = D + 4
    CW = 96
    NSLOT = 11
    LAG = 5
    CHOSEN = LAG + CH

    xbuf = nc.dram_tensor("xbuf", [SLOTS, ROW], F32).ap()
    x_t = x.rearrange("b (c p) d -> p (b c) d", p=P)
    ctx_t = ctx_in.rearrange("b (c p) d -> p (b c) d", p=P)
    out_rows = out.rearrange("b s d -> (b s) d")
    out_t = out.rearrange("b (c p) d -> p (b c) d", p=P)

    with ExitStack() as stack:
        def sb(name, shape, dt=F32):
            return stack.enter_context(nc.sbuf_tensor(name, shape, dt))

        def psum(name, shape, dt=F32):
            return stack.enter_context(nc.psum_tensor(name, shape, dt))

        def sem(name):
            return stack.enter_context(nc.semaphore(name))

        W = sb("W", [P, NSLOT, 3, G, D])
        Wflat = W[:].rearrange("p s m g d -> p s (m g d)")
        rowsX = sb("rowsX", [P, NT, ROW])
        ctxN = sb("ctxN", [P, NT, D])
        qkT = sb("qkT", [P, 2 * G, T])
        qT, kT = qkT[:, 0:G, :], qkT[:, G:2 * G, :]
        decay = sb("decay", [P, 4, NH * P])
        xn = sb("xn", [P, 2, D])
        st1 = sb("st1", [P, NT, 6])
        mv1 = sb("mv1", [P, NT, 2])
        ve = sb("ve", [P, 4, NH * H1 + CW - H1])
        vp = sb("vp", [P, 2, NH, H1])
        carried = sb("carried", [P, NH, H1])
        hs = sb("hs", [P, 4, NH, H1])
        sq = sb("sq", [P, 2, NH, HD])
        qm = sb("qm", [P, 2, G, HG, P])
        xt = sb("xt", [P, 2, D])
        xtT = sb("xtT", [P, 2, G, P])
        base = sb("base", [P, 2, D])
        state = sb("state", [P, 2, G, HG * H1])
        fresh = sb("fresh", [P, G * HG * H1])
        tok = sb("tok", [P, CH, P])
        chdec = sb("chdec", [P, B * G, 2])
        small = sb("small", [P, 6, 2, NH])
        st2 = sb("st2", [P, 2, 6])
        bcoef = sb("bcoef", [P, 2, 2, 2])
        gsb = sb("gsb", [P, CH * 2 * B * NH])
        logits = sb("logits", [P, CH, E])
        lwork = sb("lwork", [P, 4, CH, E])
        hot = sb("hot", [P, B, CH, E], BF16)
        hotsum = sb("hotsum", [P, E], BF16)
        hotpart = sb("hotpart", [P, E], BF16)
        rsm = sb("rsm", [P, 8, CH])
        slot = sb("slot", [P, NT], U32)
        wg_in = sb("wg_in", [P, 3 * G, 2, NH])
        wg = sb("wg", [P, 2 * G, CW])
        wr = sb("wr", [P, G, CW])
        bias = sb("bias", [2 * B * NH, 1])
        NC = consts.shape[1]
        cst = sb("cst", [P, NC])
        cstb = sb("cstb", [P, 2 * P], BF16)
        xinit = sb("xinit", [P, ROW])

        ident = cst[:, 0:P]
        o = P
        blockmask = cst[:, o:o + G * HG * H1]; o += G * HG * H1
        headrow = cst[:, o:o + P]; o += P
        bgmask = cst[:, o:o + B * G]; o += B * G
        rev = cst[:, o:o + E]; o += E
        tri_f = cst[:, o:o + 2 * P]; o += 2 * P
        neghalf = cst[:, o:o + 2 * NH]; o += 2 * NH
        assert o == NC
        tri, ones = cstb[:, 0:P], cstb[:, P:2 * P]

        R = B * NH
        gates_sb, logf, cumf, a_row, m_row, one_row = (
            Wflat[:, NSLOT - 2 + i // 3, (i % 3) * S:(i % 3 + 1) * S] for i in range(6))
        args = sb("args", [P, S])
        m_seq = Wflat[:, NSLOT - 5:NSLOT - 2, :].rearrange("p s n -> p (s n)")[:, 0:CH * NH * P].rearrange(
            "p (h c i) -> p h c i", h=NH, c=CH)
        LATE = 5

        pool_f = qkT[:].rearrange("p a t -> p (a t)")
        NR = 16
        f = [0]

        def cut(n):
            f[0] += n
            return pool_f[:, f[0] - n:f[0]]

        erow = cut(NR * ROW).rearrange("p (e r) -> p e r", e=NR)
        ext = cut(2 * D).rearrange("p (e r) -> p e r", e=2)
        ebase = cut(4 * D).rearrange("p (e r) -> p e r", e=4)
        eout = cut(4 * D).rearrange("p (e r) -> p e r", e=4)
        extT = cut(2 * G * CW).rearrange("p (e g c) -> p e g c", e=2, g=G)
        esil = cut(2 * G * C).rearrange("p (e g c) -> p e g c", e=2, g=G)
        ehT = cut(2 * G * C).rearrange("p (e g c) -> p e g c", e=2, g=G)

        pq = psum("pq", [P, 4, 512])
        pown = psum("pown", [P, 512])
        pearly = psum("pearly", [P, 512])
        pstate = psum("pstate", [P, 512])
        pmisc = psum("pmisc", [P, 512])
        pgate = pown[:, 0:NT * 2 * NH].rearrange("p (b c g h) -> p c g b h", b=B, c=CH, g=2)
        own = pown[:, 0:NH * H1]
        early = pearly[:, 0:NH * H1]

        def xtT_ps(n):
            return (pmisc if n <= NT - LAG else pq[:, n % 4])[:, 0:G * P]

        def log_ps(n):
            return (pmisc if n <= NT - LAG else pq[:, n % 4])[:, G * P:G * P + CW]

        cnt_ps = pmisc[:, 256 + CW:256 + CW + CH * E]

        x_in = [sem(f"x_in{b}") for b in range(B)]
        c_in = [sem(f"c_in{b}") for b in range(B)]
        cst_in, par_in, par_in2 = sem("cst_in"), sem("par_in"), sem("par_in2")
        w_in = [sem(f"w_in{s}") for s in range(NSLOT)]
        init_set, init_out = sem("init_set"), sem("init_out")
        cstb_set, ones_set = sem("cstb_set"), sem("ones_set")
        ln1_ready, xn_ready, tr1_ready, qk_copied = sem("ln1_ready"), sem("xn_ready"), sem("tr1_ready"), sem("qk_copied")
        rstd1_ready = sem("rstd1_ready")
        gates_done, gates_copied, gatesT_done, gatesT_copied = (
            sem("gates_done"), sem("gates_copied"), sem("gatesT_done"), sem("gatesT_copied"))
        softplus_ready, gate_step, args_ready, exps_ready = (
            sem("softplus_ready"), sem("gate_step"), sem("args_ready"), sem("exps_ready"))
        act_gate = sem("act_gate")
        m_ready, m_in = sem("m_ready"), [sem(f"m_in{b}") for b in range(B)]
        tokT_done, tok_ready, chsel_ready, chdec_done, chdec_ready = (
            sem("tokT_done"), sem("tok_ready"), sem("chsel_ready"), sem("chdec_done"), sem("chdec_ready"))
        mb_raw, mb_ready = sem("mb_raw"), sem("mb_ready")
        ve_ready, vp_ready = sem("ve_ready"), sem("vp_ready")
        scores_done, exp_done, c_ready = sem("scores_done"), sem("exp_done"), sem("c_ready")
        own_done, early_done, state_done, state_ready = (
            sem("own_done"), sem("early_done"), sem("state_done"), sem("state_ready"))
        fresh_ready, carried_ready, hs_ready = sem("fresh_ready"), sem("carried_ready"), sem("hs_ready")
        sq_ready, z_ready, r_ready = sem("sq_ready"), sem("z_ready"), sem("r_ready")
        norm_step, var_ready, rstd_ready, xt_ready = (
            sem("norm_step"), sem("var_ready"), sem("rstd_ready"), sem("xt_ready"))
        base_ready = sem("base_ready")
        base_out = [sem(f"base_out{i}") for i in range(2)]
        xtT_done, xtT_ready, log_done, log_ready = sem("xtT_done"), sem("xtT_ready"), sem("log_done"), sem("log_ready")
        route_step, lexp_in, lexp_ready, hot_ready, cnt_done, slot_ready = (
            sem("route_step"), sem("lexp_in"), sem("lexp_ready"), sem("hot_ready"), sem("cnt_done"), sem("slot_ready"))
        cnt_read = sem("cnt_read")
        rows_out = sem("rows_out")
        erow_in = [sem(f"erow_in{i}") for i in range(4)]
        e_xt, e_xtT_done, e_xtT, e_base = sem("e_xt"), sem("e_xtT_done"), sem("e_xtT"), sem("e_base")
        e_gu, e_sil, e_h, e_y, e_out = sem("e_gu"), sem("e_sil"), sem("e_h"), sem("e_y"), sem("e_out")
        e_stored = [sem(f"e_stored{i}") for i in range(4)]
        idset, e_pad = sem("idset"), sem("e_pad")
        zeros_set, wg_ready = sem("zeros_set"), sem("wg_ready")
        qm_in = [sem(f"qm_in{i}") for i in range(2)]
        coef_ready = sem("coef_ready")

        block = stack.enter_context(nc.Block())

        def chunk(n):
            return slice(n * P, (n + 1) * P)

        def n_state(n):
            return (n // CH) * (CH - 1) + min(n % CH + 1, CH - 1)

        @block.sync
        def _(sp):
            for b in range(B):
                sp.dma_start(rowsX[:, b * CH:(b + 1) * CH, 0:D], x_t[:, b * CH:(b + 1) * CH, :]).then_inc(x_in[b], 16)
                if b == 0:
                    sp.dma_start(cst[:], consts).then_inc(cst_in, 16)
                sp.dma_start(ctxN[:, b * CH:(b + 1) * CH, :], ctx_t[:, b * CH:(b + 1) * CH, :]).then_inc(c_in[b], 16)
                if b == 0:
                    with nc.allow_non_contiguous_dma(reason="small parameters"):
                        for i, kern in enumerate((ik, fk)):
                            sp.dma_start(wg_in[:, :, i, :], kern.rearrange("(a p) h -> p a h", p=P)).then_inc(par_in, 16)
            with nc.allow_non_contiguous_dma(reason="small parameters"):
                sp.wait_ge(zeros_set, 1)
                sp.dma_start(wr[:, :, 0:E], w_router.rearrange("(g p) e -> p g e", p=P)).then_inc(par_in2, 16)
                for i, bb in enumerate((ib, fb)):
                    for r in range(B):
                        lo = (i * B + r) * NH
                        sp.dma_start(bias[lo:lo + NH, :], bb.rearrange("(h a) -> h a", a=1)).then_inc(par_in2, 16)
            sp.wait_ge(init_set, 2)
            k = SLOTS // P
            sp.dma_start(xbuf.rearrange("(p k) r -> p k r", k=k),
                         xinit[:].unsqueeze(1).broadcast_to([P, k, ROW])).then_inc(init_out, 16)

            def load_expert(e):
                s = e % NSLOT
                for m, w in enumerate((w_gate, w_up, w_down)):
                    sp.dma_start(W[:, s, m, :, :], w[e].rearrange("(p g) f -> p g f", g=G)).then_inc(w_in[s], 16)

            for e in range(NSLOT - LATE):
                load_expert(e)
            def store_base(n):
                sp.wait_ge(base_ready, n + 1)
                sp.dma_start(out_t[:, n, :], base[:, n % 2, :]).then_inc(base_out[n % 2], 16)

            def spread_queries(n):
                if n == 0:
                    sp.wait_ge(zeros_set, 2)
                    sp.wait_ge(qk_copied, NT)
                if n >= 2:
                    sp.wait_ge(scores_done, n - 1)
                for h in range(HG):
                    r = slice(h * HD, (h + 1) * HD)
                    sp.dma_start(qm[r, n % 2, :, h, :], qT[r, :, chunk(n)]).then_inc(qm_in[n % 2], 16)

            spread_queries(0)
            spread_queries(1)
            sp.wait_ge(m_ready, 1)
            for b in range(B):
                sp.dma_start(m_seq[32 * b:32 * b + 1].rearrange("p h c i -> p h (c i)"),
                             one_row[b * NH:(b + 1) * NH, :]).then_inc(m_in[b], 16)
            for n in range(2, NT):
                spread_queries(n)
                if n >= 7:
                    store_base(n - 7)
            for n in range(NT - 7, NT):
                store_base(n)
            sp.wait_ge(mb_raw, NT)
            sp.wait_ge(exps_ready, 1)
            for e in range(NSLOT - LATE, NSLOT):
                load_expert(e)

            def load_rows(q):
                sp.dma_start(erow[0:C, 4 * q % NR:4 * q % NR + 4, :],
                             xbuf[4 * q * C:4 * (q + 1) * C, :].rearrange("(e c) r -> c e r", c=C)
                             ).then_inc(erow_in[q % 4], 16)

            sp.wait_ge(rows_out, 16 * NT)
            for q in range(NR // 4):
                load_rows(q)
            for e in range(E):
                if e % 4 == 3 and e // 4 + NR // 4 < E // 4:
                    for i in range(4):
                        sp.wait_ge(e_stored[i], 16 * (e // 4 + 1))
                    load_rows(e // 4 + NR // 4)
                if e + NSLOT < E:
                    sp.wait_ge(e_y, e + 1)
                    load_expert(e + NSLOT)
            for i in range(4):
                sp.wait_ge(e_stored[i], 16 * (E // 4))

        @block.gpsimd
        def _(pool):
            nc.gpsimd.memset(xinit[:], 0.0).then_inc(init_set, 1)
            pool.wait_ge(init_set, 1)
            nc.gpsimd.iota(xinit[:, D + 3:D + 4].bitcast(I32), pattern=[[0, 1]], base=T,
                           channel_multiplier=0).then_inc(init_set, 1)
            nc.gpsimd.iota(rowsX[:, :, D + 3].bitcast(I32), pattern=[[P, NT]], base=0,
                           channel_multiplier=1).then_inc(idset, 1)
            nc.gpsimd.memset(wr[:], 0.0).then_inc(zeros_set, 1)
            nc.gpsimd.memset(ve[:], 1.0).then_inc(ones_set, 1)
            nc.gpsimd.memset(Wflat[0:R, NSLOT - 1, 2 * S:3 * S], 1.0).then_inc(ones_set, 1)
            nc.gpsimd.memset(qm[:], 0.0).then_inc(zeros_set, 1)
            pool.wait_ge(cst_in, 16)
            for b in range(B):
                pool.wait_ge(ln1_ready, b + 1)
                v = mv1[:, b * CH:(b + 1) * CH, 1]
                nc.gpsimd.tensor_tensor(v, v, neghalf[:, 0:CH], ALU.pow).then_inc(rstd1_ready, 1)

            def broadcast_m(n, s):
                b, c = divmod(n, CH)
                pool.wait_ge(m_in[b], 16)
                if n >= 4:
                    pool.wait_ge(own_done, n - 3)
                for signal, count in ((mb_ready, n), (vp_ready, n_state(s) if s >= 0 and n > 1 else 0),
                                      (r_ready, (s - 1) // 2), (rstd_ready, (s - 2) // 2),
                                      (rows_out, 16 * CH * ((s - 3 - LAG) // CH))):
                    if count > 0:
                        pool.wait_ge(signal, count)
                v = decay[:, n % 4, :].rearrange("p (h i) -> p h i", i=P)
                nc.gpsimd.partition_broadcast(v, m_seq[32 * b:32 * b + 1, :, c, :], channels=P).then_inc(mb_raw, 1)
                pool.wait_ge(mb_raw, n + 1)
                nc.gpsimd.affine_select(out=v, in_=v, compare_op=ALU.is_ge, fill=NEG, base=0,
                                        pattern=[[0, NH], [1, P]], channel_multiplier=-1).then_inc(mb_ready, 1)

            def values(n):
                b, c = divmod(n, CH)
                pool.wait_ge(ve_ready, n + 1)
                if n_state(n) > 2:
                    pool.wait_ge(state_done, n_state(n) - 2)
                w = tok[:, c, b * NH:(b + 1) * NH].unsqueeze(2).broadcast_to([P, NH, H1])
                nc.gpsimd.tensor_tensor(vp[:, n_state(n) % 2],
                                        ve[:, n % 4, 0:NH * H1].rearrange("p (h d) -> p h d", h=NH), w,
                                        ALU.mult).then_inc(vp_ready, 1)

            pool.wait_ge(ones_set, 2)
            pool.wait_ge(zeros_set, 2)
            broadcast_m(0, 0)
            broadcast_m(1, 0)
            pool.wait_ge(tok_ready, 1)

            def scatter_rows(b):
                pool.wait_ge(slot_ready, b + 1)
                if b == 0:
                    pool.wait_ge(init_out, 16)
                    pool.wait_ge(idset, 1)
                for n in range(b * CH, (b + 1) * CH):
                    nc.gpsimd.indirect_dma_start(
                        out=xbuf, out_offset=bass.IndirectOffsetOnAxis(ap=slot[:, n:n + 1], axis=0),
                        in_=rowsX[:, n, :], in_offset=None, bounds_check=SLOTS - 1,
                        oob_is_err=False).then_inc(rows_out, 16)

            def head_scale(q):
                pool.wait_ge(z_ready, q + 1)
                nc.gpsimd.tensor_tensor(small[:, 4 + q % 2].rearrange("p c h -> p (c h)"),
                                        small[:, 2 + q % 2].rearrange("p c h -> p (c h)"), neghalf,
                                        ALU.pow).then_inc(r_ready, 1)

            def row_scale(q):
                pool.wait_ge(var_ready, q + 1)
                v = rowsX[:, 2 * q:2 * q + 2, D + 1]
                nc.gpsimd.tensor_tensor(v, v, neghalf[:, 0:2], ALU.pow).then_inc(rstd_ready, 1)

            for s in range(NT):
                if s % CH < CH - 1:
                    values(s)
                if s + 2 < NT:
                    broadcast_m(s + 2, s)
                if s >= CHOSEN + 2 and (s - CHOSEN - 2) % CH == 0:
                    scatter_rows((s - CHOSEN - 2) // CH)
                if s % 2 == 0 and s >= 2:
                    head_scale((s - 2) // 2)
                if s % 2 == 1 and s >= 3:
                    row_scale((s - 3) // 2)
            head_scale(NT // 2 - 1)
            row_scale(NT // 2 - 1)
            scatter_rows(B - 2)
            scatter_rows(B - 1)
            for i in range(2):
                pool.wait_ge(base_out[i], 16 * NT // 2)
            for e in range(E + 2):
                if e < E:
                    pool.wait_ge(e_xt, e + 1)
                    if e >= 4:
                        pool.wait_ge(e_out, e - 3)
                    nc.gpsimd.tensor_tensor(ebase[0:C, e % 4, :], erow[0:C, e % NR, 0:D], ext[0:C, e % 2, :],
                                            ALU.add).then_inc(e_base, 1)
                d = e - 2
                if d >= 0:
                    pool.wait_ge(e_out, d + 1)
                    nc.gpsimd.indirect_dma_start(
                        out=out_rows, out_offset=bass.IndirectOffsetOnAxis(
                            ap=erow[0:C, d % NR, D + 3:D + 4].bitcast(U32), axis=0),
                        in_=eout[0:C, d % 4, :], in_offset=None, bounds_check=T - 1,
                        oob_is_err=False).then_inc(e_stored[d % 4], 16)

        @block.scalar
        def _(act):
            for n in range(NT):
                act.wait_ge(tr1_ready, n + 1)
                nc.scalar.copy(qkT[:, :, chunk(n)],
                               pq[:, n % 4, :].rearrange("p (a t) -> p a t", t=P)).then_inc(qk_copied, 1)
            act.wait_ge(gatesT_copied, 1)
            nc.scalar.activation(logf[0:R, :], gates_sb[R:2 * R, :], ACT.Abs).then_inc(act_gate, 1)
            act.wait_ge(act_gate, 1)
            nc.scalar.activation(logf[0:R, :], logf[0:R, :], ACT.Exp, scale=-1.0).then_inc(act_gate, 1)
            act.wait_ge(act_gate, 2)
            nc.scalar.activation(logf[0:R, :], logf[0:R, :], ACT.Ln, bias=1.0).then_inc(softplus_ready, 1)
            act.wait_ge(args_ready, 1)
            nc.scalar.activation(args[0:3 * R, :], args[0:3 * R, :], ACT.Exp).then_inc(exps_ready, 1)
            act.wait_ge(tokT_done, 1)
            nc.scalar.copy(tok[:], pstate[:].rearrange("p (c r) -> p c r", c=CH)).then_inc(tok_ready, 1)
            act.wait_ge(tok_ready, 1)

            def values(n):
                if n % CH == 0:
                    act.wait_ge(c_in[n // CH], 16)
                if n >= 4:
                    act.wait_ge(own_done, n - 3)
                    act.wait_ge(vp_ready, n_state(n - 4))
                nc.scalar.copy(ve[:, n % 4, 0:NH * H1].rearrange("p (h d) -> p h d", h=NH)[:, :, 0:HD],
                               ctxN[:, n, :].rearrange("p (h d) -> p h d", h=NH)).then_inc(ve_ready, 1)

            act.wait_ge(ones_set, 1)
            def decay_of(n):
                b, c = divmod(n, CH)
                act.wait_ge(mb_ready, n + 1)
                for h in range(NH):
                    v = decay[:, n % 4, h * P:(h + 1) * P]
                    last = nc.scalar.activation(v, v, ACT.Exp,
                                                bias=tok[:, c, 3 * R + b * NH + h:3 * R + b * NH + h + 1])
                last.then_inc(exp_done, 1)

            def squares(q):
                act.wait_ge(hs_ready, 2 * q + 2)
                if q >= 1:
                    act.wait_ge(z_ready, q)
                nc.scalar.activation(sq[:], hs[:, 2 * (q % 2):2 * (q % 2) + 2, :, 0:HD], ACT.Square,
                                     scale=float(HD) ** -0.5).then_inc(sq_ready, 1)

            def copy_x1(n):
                act.wait_ge(xtT_done, n + 1)
                if n >= 2:
                    act.wait_ge(log_done, n - 1)
                nc.scalar.copy(xtT[:, n % 2], xtT_ps(n).rearrange("p (g t) -> p g t", g=G)).then_inc(xtT_ready, 1)

            def base_rows(n):
                act.wait_ge(coef_ready, n // 2 + 1)
                if n >= 2:
                    act.wait_ge(base_out[n % 2], 16 * (n // 2))
                nc.scalar.activation(base[:, n % 2, :], rowsX[:, n, 0:D], ACT.Identity,
                                     bias=bcoef[:, n // 2 % 2, n % 2, 1:2],
                                     scale=bcoef[:, n // 2 % 2, n % 2, 0:1]).then_inc(base_ready, 1)

            def copy_logits(n):
                act.wait_ge(log_done, n + 1)
                if n >= CH and n % CH == 0:
                    act.wait_ge(hot_ready, n // CH)
                nc.scalar.copy(logits[:, n % CH, :], log_ps(n)[:, 0:E]).then_inc(log_ready, 1)

            def exp_logits(b):
                act.wait_ge(lexp_in, b + 1)
                nc.scalar.activation(lwork[:, 1], lwork[:, 0], ACT.Exp).then_inc(lexp_ready, 1)

            values(0)
            values(1)
            decay_of(0)
            for s in range(NT):
                if s + 1 < NT:
                    decay_of(s + 1)
                if s + 2 < NT:
                    values(s + 2)
                if s >= LAG:
                    copy_x1(s - LAG)
                    base_rows(s - LAG)
                if s >= CHOSEN and (s - CHOSEN) % CH == 0:
                    exp_logits((s - CHOSEN) // CH)
                if s % 2 == 0 and s >= 2:
                    squares((s - 2) // 2)
                if s >= LAG:
                    copy_logits(s - LAG)
            n = NT - LAG
            copy_x1(n)
            squares(NT // 2 - 1)
            base_rows(n)
            copy_logits(n)
            copy_x1(n + 1)
            copy_x1(n + 2)
            exp_logits(B - 2)
            copy_logits(n + 1)
            copy_logits(n + 2)
            base_rows(n + 1)
            base_rows(n + 2)
            copy_x1(n + 3)
            copy_x1(n + 4)
            copy_logits(n + 3)
            copy_logits(n + 4)
            exp_logits(B - 1)
            base_rows(n + 3)
            base_rows(n + 4)
            for e in range(E):
                act.wait_ge(e_gu, e + 1)
                if e >= 2:
                    act.wait_ge(e_h, e - 1)
                nc.scalar.activation(esil[:, e % 2],
                                     pq[:, e % 2, 0:G * CW].rearrange("p (g c) -> p g c", g=G)[:, :, 0:C],
                                     ACT.Silu).then_inc(e_sil, 1)

        @block.tensor
        def _(pe):
            def gates(n):
                pe.wait_ge(qk_copied, n + 1)
                for i in range(2 * G):
                    last = nc.tensor.matmul(pown[:, n * 2 * NH:n * 2 * NH + CW], qkT[:, i, chunk(n)], wg[:, i, :],
                                            start=(i == 0), stop=(i == 2 * G - 1))
                last.then_inc(gates_done, 1)

            pe.wait_ge(cst_in, 16)
            for n in range(NT):
                if n % CH == 0:
                    pe.wait_ge(c_in[n // CH], 16)
                pe.wait_ge(xn_ready, n + 1)
                if n >= 4:
                    pe.wait_ge(qk_copied, n - 3)
                for i in range(2 * G):
                    src = xn[:, n % 2, i * P:(i + 1) * P] if i < G else ctxN[:, n, (i - G) * P:(i - G + 1) * P]
                    last = nc.tensor.transpose(pq[:, n % 4, i * P:(i + 1) * P], src, ident)
                last.then_inc(tr1_ready, 1)
                if n == 1:
                    pe.wait_ge(wg_ready, 3)
                if n >= 1:
                    gates(n - 1)
            gates(NT - 1)
            pe.wait_ge(gates_copied, 1)
            for c in range(CH):
                last = nc.tensor.transpose(pearly[0:2 * R, chunk(c)], gsb[:, c * 2 * R:(c + 1) * 2 * R], ident)
            last.then_inc(gatesT_done, 1)
            pe.wait_ge(exps_ready, 1)
            pe.wait_ge(args_ready, 2)
            for c in range(CH):
                last = nc.tensor.transpose(pstate[:, chunk(c)], args[:, chunk(c)], ident)
            last.then_inc(tokT_done, 1)
            pe.wait_ge(chsel_ready, 1)
            nc.tensor.matmul(pmisc[:, 0:2 * B * G], headrow[R:2 * R, :], gsb[R:2 * R, 0:2 * B * G],
                             start=True, stop=True).then_inc(chdec_done, 1)

            def scores(n):
                pe.wait_ge(qm_in[n % 2], 16 * HG * (n // 2 + 1))
                if n >= 2:
                    pe.wait_ge(c_ready, n - 1)
                for g in range(G):
                    last = nc.tensor.matmul(pq[:, 2 * (n % 2) + g, :], kT[:, g, chunk(n)],
                                            qm[:, n % 2, g].rearrange("p h i -> p (h i)"), start=True, stop=True)
                last.then_inc(scores_done, 1)

            def outputs(n):
                c = n % CH
                if c > 0:
                    pe.wait_ge(state_ready, n_state(n - 1))
                    if n_state(n - 1) > 1:
                        pe.wait_ge(carried_ready, n_state(n - 1) - 1)
                    for g in range(G):
                        w = HG * H1
                        last = nc.tensor.matmul(early[:, g * w:(g + 1) * w], qT[:, g, chunk(n)],
                                                state[:, n_state(n - 1) % 2, g, :], start=True, stop=True)
                    last.then_inc(early_done, 1)
                pe.wait_ge(c_ready, n + 1)
                pe.wait_ge(ve_ready, n + 1)
                if n == 0:
                    pe.wait_ge(gates_copied, 1)
                else:
                    pe.wait_ge(hs_ready, n)
                for h in range(NH):
                    last = nc.tensor.matmul(pown[:, h * H1:h * H1 + CW], decay[:, n % 4, h * P:(h + 1) * P],
                                            ve[:, n % 4, h * H1:h * H1 + CW], start=True, stop=True)
                last.then_inc(own_done, 1)

            def state_sum(n):
                k = n_state(n)
                pe.wait_ge(vp_ready, k)
                if k > 1:
                    pe.wait_ge(fresh_ready, k - 1)
                else:
                    pe.wait_ge(tok_ready, 1)
                w = HG * H1
                for g in range(G):
                    last = nc.tensor.matmul(pstate[:, g * w:(g + 1) * w], ctxN[:, n, g * P:(g + 1) * P],
                                            vp[:, k % 2, g * HG:(g + 1) * HG, :].rearrange("p h d -> p (h d)"),
                                            start=True, stop=True)
                last.then_inc(state_done, 1)

            def router(n):
                pe.wait_ge(xtT_ready, n + 1)
                if n == 0:
                    pe.wait_ge(par_in2, 16 * (1 + 2 * B))
                for g in range(G):
                    last = nc.tensor.matmul(log_ps(n), xtT[:, n % 2, g, :], wr[:, g, :], start=(g == 0),
                                            stop=(g == G - 1))
                last.then_inc(log_done, 1)

            def counts(b):
                pe.wait_ge(hot_ready, b + 1)
                for t in range(CH):
                    o_ = cnt_ps[:, t * E:(t + 1) * E]
                    nc.tensor.matmul(o_, ones, hotsum[:], start=True, stop=False)
                    for u in range(t):
                        nc.tensor.matmul(o_, ones, hot[:, b, u, :], start=False, stop=False)
                    last = nc.tensor.matmul(o_, tri, hot[:, b, t, :], start=False, stop=True)
                last.then_inc(cnt_done, 1)

            def transpose_x1(n):
                pe.wait_ge(xt_ready, n + 1)
                if n == 0:
                    pe.wait_ge(chdec_ready, 1)
                for g in range(G):
                    last = nc.tensor.transpose(xtT_ps(n)[:, g * P:(g + 1) * P], xt[:, n % 2, g * P:(g + 1) * P], ident)
                last.then_inc(xtT_done, 1)

            for s in range(NT):
                scores(s)
                if s >= LAG:
                    if s > LAG:
                        pe.wait_ge(log_ready, s - LAG)
                    if s > CHOSEN:
                        pe.wait_ge(cnt_read, (s - CHOSEN - 1) // CH + 1)
                    transpose_x1(s - LAG)
                if s >= 1:
                    outputs(s - 1)
                if s % CH < CH - 1:
                    state_sum(s)
                if s >= CHOSEN and (s - CHOSEN) % CH == 0:
                    pe.wait_ge(xtT_ready, s - LAG + 1)
                    counts((s - CHOSEN) // CH)
                if s >= LAG:
                    router(s - LAG)
            n = NT - LAG
            pe.wait_ge(log_ready, n)
            transpose_x1(n)
            outputs(NT - 1)
            router(n)
            pe.wait_ge(c_ready, NT)
            transpose_x1(n + 1)
            transpose_x1(n + 2)
            pe.wait_ge(log_ready, n + 1)
            counts(B - 2)
            router(n + 1)
            router(n + 2)
            transpose_x1(n + 3)
            transpose_x1(n + 4)
            router(n + 3)
            router(n + 4)
            pe.wait_ge(cnt_read, B - 1)
            counts(B - 1)

            def e_transpose(e):
                pe.wait_ge(e_xt, e + 1)
                if e >= 2:
                    pe.wait_ge(e_xtT, e - 1)
                bank = (pown, pearly)[e % 2]
                v = ext[0:C, e % 2, :].rearrange("c (p g) -> c g p", g=G)
                for g in range(G):
                    last = nc.tensor.transpose(bank[:, g * C:(g + 1) * C], v[:, g, :], ident[0:C, 0:C])
                last.then_inc(e_xtT_done, 1)

            def e_gate_up(e):
                s = e % NSLOT
                pe.wait_ge(w_in[s], 48 * (e // NSLOT + 1))
                pe.wait_ge(e_pad, 1)
                pe.wait_ge(e_xtT, e + 1)
                if e >= 2:
                    pe.wait_ge(e_h, e - 1)
                for m in range(2):
                    for j in range(G):
                        o_ = pq[:, e % 2, (m * G + j) * CW:(m * G + j + 1) * CW]
                        for g in range(G):
                            w = W[:, s, m, g, :].rearrange("p (m j) -> p j m", j=G)[:, j, :]
                            last = nc.tensor.matmul(o_, w, extT[:, e % 2, g, :], start=(g == 0), stop=(g == G - 1))
                last.then_inc(e_gu, 1)

            def e_down(e):
                pe.wait_ge(e_h, e + 1)
                if e >= 2:
                    pe.wait_ge(e_out, e - 1)
                for j in range(G):
                    last = nc.tensor.matmul(pq[0:C, 2 + e % 2, 0:D], ehT[:, e % 2, j, :], W[:, e % NSLOT, 2, j, :],
                                            start=(j == 0), stop=(j == G - 1))
                last.then_inc(e_y, 1)

            e_transpose(0)
            for e in range(E):
                if e + 1 < E:
                    e_transpose(e + 1)
                e_gate_up(e)
                if e >= 1:
                    e_down(e - 1)
            e_down(E - 1)

        @block.vector
        def _(dve):
            V = nc.vector
            V.memset(wg[:], 0.0).then_inc(wg_ready, 1)
            V.memset(hotsum[:], 0.0).then_inc(cstb_set, 1)

            def xn_of(b):
                dve.wait_ge(rstd1_ready, b + 1)
                for n in range(b * CH, (b + 1) * CH):
                    if n >= 2:
                        dve.wait_ge(tr1_ready, n - 1)
                    V.tensor_scalar(xn[:, n % 2, :], rowsX[:, n, 0:D], mv1[:, n, 0:1], mv1[:, n, 1:2],
                                    ALU.subtract, ALU.mult).then_inc(xn_ready, 1)

            for b in range(B):
                dve.wait_ge(x_in[b], 16)
                for n in range(b * CH, (b + 1) * CH):
                    V.bn_stats(st1[:, n, :], rowsX[:, n, 0:D]).then_inc(gate_step, 1)
                for n in range(b * CH, (b + 1) * CH):
                    dve.wait_ge(gate_step, CH * 2 * b + b + n - b * CH + 1)
                    V.bn_aggr(mv1[:, n, :], st1[:, n, :]).then_inc(gate_step, 1)
                dve.wait_ge(gate_step, b * (2 * CH + 1) + 2 * CH)
                v = mv1[:, b * CH:(b + 1) * CH, 1]
                V.tensor_scalar(v, v, LN_EPS, None, ALU.add).then_inc(ln1_ready, 1)
                V.engine_nop().then_inc(gate_step, 1)
                if b >= 1:
                    xn_of(b - 1)
                else:
                    dve.wait_ge(wg_ready, 1)
                    dve.wait_ge(par_in, 16 * 2)
                    wgs = wg[:, :, 0:2 * NH].rearrange("p a (i h) -> p a i h", i=2)
                    V.tensor_copy(wgs[:, 0:G], wg_in[:, 0:G]).then_inc(wg_ready, 1)
                    V.tensor_tensor(wgs[:, G:2 * G], wg_in[:, G:2 * G], wg_in[:, 2 * G:3 * G],
                                    ALU.add).then_inc(wg_ready, 1)
                    dve.wait_ge(cst_in, 16)
                    V.tensor_copy(cstb[:], tri_f).then_inc(cstb_set, 1)
            xn_of(B - 1)
            gs = [B * (2 * CH + 1)]

            def step(ins):
                gs[0] += 1
                ins.then_inc(gate_step, 1)
                dve.wait_ge(gate_step, gs[0])

            dve.wait_ge(gates_done, NT)
            for c in range(CH):
                last = V.tensor_copy(gsb[:, c * 2 * R:(c + 1) * 2 * R].rearrange("p (g b h) -> p g b h", g=2, b=B),
                                     pgate[:, c])
            last.then_inc(gates_copied, 1)
            dve.wait_ge(gatesT_done, 1)
            dve.wait_ge(par_in2, 16 * (1 + 2 * B))
            V.tensor_scalar(gates_sb[0:2 * R, :], pearly[0:2 * R, :], bias[:, 0:1], None,
                            ALU.add).then_inc(gatesT_copied, 1)
            dve.wait_ge(gatesT_copied, 1)
            step(V.tensor_scalar(cumf[0:R, :], gates_sb[R:2 * R, :], 0.0, None, ALU.min))
            dve.wait_ge(softplus_ready, 1)
            step(V.tensor_tensor(logf[0:R, :], cumf[0:R, :], logf[0:R, :], ALU.subtract))
            dve.wait_ge(ones_set, 2)
            step(V.tensor_tensor_scan(cumf[0:R, :], one_row[0:R, :], logf[0:R, :], 0.0, ALU.mult, ALU.add))
            step(V.tensor_tensor(a_row[0:R, :], gates_sb[0:R, :], cumf[0:R, :], ALU.subtract))
            step(V.tensor_tensor_scan(m_row[0:R, :], a_row[0:R, :], a_row[0:R, :], -3.0e38, ALU.max, ALU.max))
            V.tensor_scalar(one_row[0:R, :], m_row[0:R, :], -1.0, None, ALU.mult).then_inc(m_ready, 1)
            mr = m_row[0:R, :].rearrange("p (c i) -> p c i", c=CH)
            ar = a_row[0:R, :].rearrange("p (c i) -> p c i", c=CH)
            ends = mr[:, :, P - 1:P].broadcast_to([R, CH, P])
            A = args[:].rearrange("p (c i) -> p c i", c=CH)
            V.tensor_tensor(A[0:R], ar, ends, ALU.subtract)
            V.memset(A[R:2 * R, 0, :], 0.0)
            V.tensor_tensor(A[R:2 * R, 1:CH, :], mr[:, 0:CH - 1, P - 1:P].broadcast_to([R, CH - 1, P]), mr[:, 1:CH, :],
                            ALU.subtract)
            V.scalar_tensor_tensor(out=args[2 * R:3 * R, :], in0=cumf[0:R, :], scalar=-1.0, in1=m_row[0:R, :],
                                   op0=ALU.mult, op1=ALU.subtract).then_inc(args_ready, 1)
            V.tensor_copy(args[3 * R:4 * R, :], a_row[0:R, :]).then_inc(args_ready, 1)
            dve.wait_ge(exps_ready, 1)
            sel = gsb[R:2 * R, 0:2 * B * G].rearrange("p (g k) -> p g k", k=2)
            V.tensor_tensor(sel, bgmask[R:2 * R, :].unsqueeze(2).broadcast_to([R, B * G, 2]),
                            A[R:2 * R, 1:3, P - 1:P].rearrange("p a b -> p b a").broadcast_to([R, B * G, 2]),
                            ALU.mult).then_inc(chsel_ready, 1)
            dve.wait_ge(chdec_done, 1)
            V.tensor_copy(chdec[:], pmisc[:, 0:2 * B * G].rearrange("p (g k) -> p g k", k=2)).then_inc(chdec_ready, 1)
            dve.wait_ge(tok_ready, 1)
            dve.wait_ge(chdec_ready, 1)

            def decay_scores(n):
                dve.wait_ge(scores_done, n + 1)
                dve.wait_ge(exp_done, n + 1)
                V.scalar_tensor_tensor(out=decay[:, n % 4, :],
                                       in0=pq[:, 2 * (n % 2):2 * (n % 2) + 2, :].rearrange("p g i -> p (g i)"),
                                       scalar=float(HD) ** -0.5, in1=decay[:, n % 4, :],
                                       op0=ALU.mult, op1=ALU.mult).then_inc(c_ready, 1)

            def combine(n):
                b, c = divmod(n, CH)
                if n >= 4:
                    dve.wait_ge(norm_step, n // 2 - 1)
                ow = own.rearrange("p (h d) -> p h d", h=NH)
                if c > 0:
                    w = tok[:, c, R + b * NH:R + (b + 1) * NH].unsqueeze(2).broadcast_to([P, NH, H1])
                    dve.wait_ge(early_done, n_state(n - 1))
                    V.tensor_tensor(carried[:], early.rearrange("p (h d) -> p h d", h=NH), w,
                                    ALU.mult).then_inc(carried_ready, 1)
                    dve.wait_ge(carried_ready, n_state(n - 1))
                    dve.wait_ge(own_done, n + 1)
                    V.tensor_tensor(hs[:, n % 4], ow, carried[:], ALU.add).then_inc(hs_ready, 1)
                else:
                    dve.wait_ge(own_done, n + 1)
                    V.tensor_copy(hs[:, n % 4], ow).then_inc(hs_ready, 1)

            def normalizer(q):
                b, c = divmod(2 * q, CH)
                dve.wait_ge(hs_ready, 2 * q + 2)
                total = hs[:, 2 * (q % 2):2 * (q % 2) + 2, :, HD]
                n0 = small[:, 0]
                link(V.scalar_tensor_tensor(out=n0, in0=total, scalar=-1.0, in1=total, op0=ALU.mult, op1=ALU.max))
                link(V.tensor_tensor(n0, n0, tok[:, c:c + 2, 2 * R + b * NH:2 * R + (b + 1) * NH], ALU.max))
                link(V.tensor_scalar(n0, n0, NORM_EPS, None, ALU.add))
                link(V.tensor_tensor(n0, n0, n0, ALU.mult))
                dve.wait_ge(sq_ready, q + 1)
                link(V.tensor_reduce(small[:, 1], sq[:], AX_X, ALU.add))
                if q >= 2:
                    dve.wait_ge(r_ready, q - 1)
                V.scalar_tensor_tensor(out=small[:, 2 + q % 2], in0=n0, scalar=1e-6, in1=small[:, 1],
                                       op0=ALU.mult, op1=ALU.add).then_inc(z_ready, 1)

            links = [0]

            def link(ins):
                links[0] += 1
                ins.then_inc(route_step, 1)
                dve.wait_ge(route_step, links[0])

            def update_state(n):
                k = n_state(n)
                b, c = divmod(n, CH)
                dve.wait_ge(state_done, k)
                if c == 0:
                    if k > 1:
                        dve.wait_ge(early_done, k - 1)
                    V.tensor_tensor(state[:, k % 2].rearrange("p g w -> p (g w)"), pstate[:, 0:G * HG * H1],
                                    blockmask, ALU.mult).then_inc(fresh_ready, 1)
                    dve.wait_ge(fresh_ready, k)
                    V.engine_nop().then_inc(state_ready, 1)
                    return
                V.tensor_tensor(fresh[:], pstate[:, 0:G * HG * H1], blockmask, ALU.mult).then_inc(fresh_ready, 1)
                dve.wait_ge(fresh_ready, k)
                dve.wait_ge(early_done, max(1, k - 2))
                w = HG * H1
                for g in range(G):
                    last = V.scalar_tensor_tensor(out=state[:, k % 2, g, :], in0=state[:, (k - 1) % 2, g, :],
                                                  scalar=chdec[:, b * G + g, c - 1:c], in1=fresh[:, g * w:(g + 1) * w],
                                                  op0=ALU.mult, op1=ALU.add)
                last.then_inc(state_ready, 1)

            def residual(q):
                dve.wait_ge(r_ready, q + 1)
                r = small[:, 4 + q % 2].rearrange("p c h -> p (c h)").unsqueeze(2).broadcast_to([P, 2 * NH, HD])
                hv = hs[:, 2 * (q % 2):2 * (q % 2) + 2].rearrange("p c h d -> p (c h) d")[:, :, 0:HD]
                V.tensor_tensor(hv, hv, r, ALU.mult).then_inc(norm_step, 1)
                dve.wait_ge(norm_step, q + 1)
                xv = rowsX[:, 2 * q:2 * q + 2, 0:D]
                x3 = xv.rearrange("p c (h d) -> p c h d", h=NH)
                link(V.tensor_tensor(x3, x3, hs[:, 2 * (q % 2):2 * (q % 2) + 2, :, 0:HD], ALU.add))
                V.bn_stats(st2[:, 0, :], xv[:, 0])
                link(V.bn_stats(st2[:, 1, :], xv[:, 1]))
                V.bn_aggr(rowsX[:, 2 * q, D:D + 2], st2[:, 0, :])
                link(V.bn_aggr(rowsX[:, 2 * q + 1, D:D + 2], st2[:, 1, :]))
                v = rowsX[:, 2 * q:2 * q + 2, D + 1]
                V.tensor_scalar(v, v, LN_EPS, None, ALU.add).then_inc(var_ready, 1)

            def norm_x1(q):
                dve.wait_ge(rstd_ready, q + 1)
                if q >= 1:
                    dve.wait_ge(xtT_done, 2 * q)
                for n in (2 * q, 2 * q + 1):
                    V.tensor_scalar(xt[:, n % 2, :], rowsX[:, n, 0:D], rowsX[:, n, D:D + 1],
                                    rowsX[:, n, D + 1:D + 2], ALU.subtract, ALU.mult).then_inc(xt_ready, 1)
                if q >= 2:
                    dve.wait_ge(base_ready, 2 * q - 2)
                mean, rstd = (rowsX[:, 2 * q:2 * q + 2, D + i] for i in range(2))
                V.tensor_scalar(bcoef[:, q % 2, :, 0], rstd, 1.0, None, ALU.add)
                V.scalar_tensor_tensor(out=bcoef[:, q % 2, :, 1], in0=mean, scalar=-1.0, in1=rstd,
                                       op0=ALU.mult, op1=ALU.mult).then_inc(coef_ready, 1)

            def choose(b):
                dve.wait_ge(log_ready, (b + 1) * CH)
                mx, g3, fm = rsm[:, 0, :], rsm[:, 1, :], rsm[:, 2, :]

                def wide(v):
                    return v.unsqueeze(2).broadcast_to([P, CH, E])
                link(V.tensor_reduce(mx, logits[:], AX_X, ALU.max))
                V.tensor_tensor(lwork[:, 0], logits[:], wide(mx), ALU.subtract).then_inc(lexp_in, 1)
                dve.wait_ge(lexp_in, b + 1)
                link(V.scalar_tensor_tensor(out=lwork[:, 2], in0=lwork[:, 0], scalar=0.0,
                                            in1=rev.unsqueeze(1).broadcast_to([P, CH, E]), op0=ALU.is_ge, op1=ALU.mult))
                link(V.tensor_reduce(fm, lwork[:, 2], AX_X, ALU.max))
                link(V.tensor_tensor(hot[:, b], lwork[:, 2], wide(fm), ALU.is_equal))
                V.engine_nop().then_inc(hot_ready, 1)
                dve.wait_ge(lexp_ready, b + 1)
                link(V.tensor_reduce(g3, lwork[:, 1], AX_X, ALU.add))
                link(V.reciprocal(rowsX[:, b * CH:(b + 1) * CH, D + 2], g3))

            def place(b):
                fm, pos, over, sl = (rsm[:, i, :] for i in range(2, 6))
                dve.wait_ge(cnt_done, b + 1)
                V.tensor_tensor(lwork[:, 3], cnt_ps.rearrange("p (t e) -> p t e", t=CH), hot[:, b],
                                ALU.mult).then_inc(cnt_read, 1)
                dve.wait_ge(cnt_read, b + 1)
                link(V.tensor_reduce(pos, lwork[:, 3], AX_X, ALU.add))
                link(V.tensor_scalar(over, pos, float(C), float(2 * SLOTS), ALU.is_ge, ALU.mult))
                link(V.scalar_tensor_tensor(out=sl, in0=fm, scalar=-float(C), in1=pos, op0=ALU.mult, op1=ALU.add))
                link(V.tensor_tensor(sl, sl, over, ALU.add))
                V.tensor_scalar(slot[:, b * CH:(b + 1) * CH], sl, float(E * C), None, ALU.add).then_inc(slot_ready, 1)
                if b + 1 < B:
                    with nc.allow_low_precision(reason="counts up to 16 are exact in bfloat16"):
                        link(V.tensor_reduce(hotpart[:], hot[:, b].rearrange("p t e -> p e t"), AX_X, ALU.add))
                    link(V.tensor_tensor(hotsum[:], hotsum[:], hotpart[:], ALU.add))

            dve.wait_ge(cstb_set, 2)
            for s in range(NT):
                if s > CHOSEN and (s - CHOSEN - 1) % CH == 0:
                    dve.wait_ge(log_ready, s - LAG)
                    place((s - CHOSEN - 1) // CH)
                decay_scores(s)
                if s >= CHOSEN and (s - CHOSEN) % CH == 0:
                    choose((s - CHOSEN) // CH)
                if s % CH < CH - 1:
                    update_state(s)
                if s >= 1:
                    combine(s - 1)
                if s % 2 == 0 and s >= 2:
                    normalizer((s - 2) // 2)
                if s % 2 == 0 and s >= 4:
                    norm_x1((s - 4) // 2)
                if s % 2 == 1 and s >= 3:
                    residual((s - 3) // 2)
            combine(NT - 1)
            normalizer(NT // 2 - 1)
            norm_x1(NT // 2 - 2)
            choose(B - 2)
            place(B - 2)
            residual(NT // 2 - 1)
            norm_x1(NT // 2 - 1)
            choose(B - 1)
            place(B - 1)

            def e_norm(e):
                if e % 4 == 0:
                    dve.wait_ge(erow_in[e // 4 % 4], 16 * (e // NR + 1))
                if e >= 2:
                    dve.wait_ge(e_xtT_done, e - 1)
                    dve.wait_ge(e_base, e - 1)
                r = erow[0:C, e % NR, :]
                V.tensor_scalar(ext[0:C, e % 2, :], r[:, 0:D], r[:, D:D + 1], r[:, D + 1:D + 2],
                                ALU.subtract, ALU.mult).then_inc(e_xt, 1)

            def e_evac(e):
                dve.wait_ge(e_xtT_done, e + 1)
                if e >= 2:
                    dve.wait_ge(e_gu, e - 1)
                V.tensor_copy(extT[:, e % 2, :, 0:C], (pown, pearly)[e % 2][:, 0:G * C].rearrange(
                    "p (g c) -> p g c", g=G)).then_inc(e_xtT, 1)

            def e_mul(e):
                dve.wait_ge(e_sil, e + 1)
                if e >= 2:
                    dve.wait_ge(e_y, e - 1)
                V.tensor_tensor(ehT[:, e % 2],
                                pq[:, e % 2, G * CW:2 * G * CW].rearrange("p (g c) -> p g c", g=G)[:, :, 0:C],
                                esil[:, e % 2], ALU.mult).then_inc(e_h, 1)

            def e_combine(e):
                dve.wait_ge(e_y, e + 1)
                dve.wait_ge(e_base, e + 1)
                if e >= 4:
                    dve.wait_ge(e_stored[e % 4], 16 * (e // 4))
                V.scalar_tensor_tensor(out=eout[0:C, e % 4, :], in0=pq[0:C, 2 + e % 2, 0:D],
                                       scalar=erow[0:C, e % NR, D + 2:D + 3], in1=ebase[0:C, e % 4, :],
                                       op0=ALU.mult, op1=ALU.add).then_inc(e_out, 1)

            dve.wait_ge(own_done, NT)
            V.memset(extT[:, :, :, C:CW], 0.0).then_inc(e_pad, 1)
            e_norm(0)
            e_evac(0)
            e_norm(1)
            for e in range(E):
                if e + 1 < E:
                    e_evac(e + 1)
                if e + 2 < E:
                    e_norm(e + 2)
                e_mul(e)
                if e >= 1:
                    e_combine(e - 1)
            e_combine(E - 1)


_INS = ['x', 'ctx_1024', 'L0_xattn_igate_kernel', 'L0_xattn_igate_bias', 'L0_xattn_fgate_kernel',
        'L0_xattn_fgate_bias', 'L0_ffn_w_router', 'L0_ffn_w_gate', 'L0_ffn_w_up', 'L0_ffn_w_down']


def shape_constants(B, D, NH, E):
    import numpy as np
    HD = D // NH
    G, HG, H1 = D // P, P // HD, HD + 1
    R = B * NH
    p = np.arange(P)
    ident = np.eye(P)
    head = np.repeat(np.arange(HG), H1)
    blockmask = np.tile((p[:, None] // HD == head[None, :]) * HD ** -0.5, (1, G))
    r = p - R
    headrow = (r[:, None] % HG == p[None, :] // HD) * 1.0
    bgmask = (r[:, None] // HG == np.arange(B * G)[None, :]) * 1.0
    rev = np.tile(E - np.arange(E), (P, 1))
    before = (p[:, None] < p[None, :]) * 1.0
    return np.concatenate([ident, blockmask, headrow, bgmask, rev, before, np.ones((P, P)),
                           np.full((P, 2 * NH), -0.5)], axis=1).astype(np.float32)


def kernel(**inputs):
    import numpy as _np
    import concourse.bacc as _bacc
    from concourse import mybir as _mybir
    from concourse.bass_utils import run_bass_kernel_spmd as _run

    nc = _bacc.Bacc("TRN2", target_bir_lowering=False, num_devices=1)
    arrays, args = {}, []
    for name in _INS:
        a = _np.ascontiguousarray(inputs[name])
        arrays[f"in_{name}_dram"] = a
        args.append(nc.dram_tensor(f"in_{name}_dram", a.shape, _mybir.dt.from_np(a.dtype), kind="ExternalInput").ap())
    b, s, d = inputs['x'].shape
    c = shape_constants(b, d, inputs['L0_xattn_igate_kernel'].shape[1], inputs['L0_ffn_w_gate'].shape[0])
    arrays["in_consts_dram"] = c
    args.append(nc.dram_tensor("in_consts_dram", c.shape, _mybir.dt.from_np(c.dtype), kind="ExternalInput").ap())
    args.append(nc.dram_tensor("out_0_dram", (b, s, d), _mybir.dt.float32, kind="ExternalOutput").ap())
    build(nc, *args)
    r = _run(nc, [arrays], core_ids=[0])
    return r.results[0]["out_0_dram"]
```

```python
from contextlib import ExitStack

import concourse.bass as bass
from concourse import mybir

ALU = mybir.AluOpType
ACT = mybir.ActivationFunctionType
F32 = mybir.dt.float32
BF16 = mybir.dt.bfloat16
I32 = mybir.dt.int32
U32 = mybir.dt.uint32
AX_X = mybir.AxisListType.X

P = 128
NEG = -1.0e30
LN_EPS = 1e-5
NORM_EPS = 1e-6


def build(nc, x, ctx_in, ik, ib, fk, fb, w_router, w_gate, w_up, w_down, consts, out):
    B, S, D = x.shape
    NH = ik.shape[1]
    HD = D // NH
    H1 = HD + 1
    CH = S // P
    NT = B * CH
    G = D // P
    HG = P // HD
    E = w_gate.shape[0]
    T = B * S
    C = -(-5 * T // (4 * E))
    SLOTS = E * C
    ROW = D + 4
    CW = 96
    HB = B // 2
    HN = NT // 2
    RH = HB * NH
    R = 32
    LOADS = [(0, 2), (2, CH)] + [(b * CH, (b + 1) * CH) for b in range(1, B)]
    LOAD_AT = {a: i for i, (a, _) in enumerate(LOADS)}
    NSLOT = 11
    LAG = 5
    CHOSEN = LAG + CH + 1

    xbuf = nc.dram_tensor("xbuf", [SLOTS, ROW], F32).ap()
    x_t = x.rearrange("b (c p) d -> p (b c) d", p=P)
    ctx_t = ctx_in.rearrange("b (c p) d -> p (b c) d", p=P)
    out_rows = out.rearrange("b s d -> (b s) d")
    out_t = out.rearrange("b (c p) d -> p (b c) d", p=P)

    with ExitStack() as stack:
        def sb(name, shape, dt=F32):
            return stack.enter_context(nc.sbuf_tensor(name, shape, dt))

        def psum(name, shape, dt=F32):
            return stack.enter_context(nc.psum_tensor(name, shape, dt))

        def sem(name):
            return stack.enter_context(nc.semaphore(name))

        W = sb("W", [P, NSLOT, 3, G, D])
        Wflat = W[:].rearrange("p s m g d -> p s (m g d)")
        rowsX = sb("rowsX", [P, NT, ROW])
        ctxN = sb("ctxN", [P, NT, D])
        qkT = sb("qkT", [P, 2 * G, T])
        qT, kT = qkT[:, 0:G, :], qkT[:, G:2 * G, :]
        decay = sb("decay", [P, 5, NH * P])
        xn = decay[:, 4, :].rearrange("p (n d) -> p n d", d=D)
        st1 = sb("st1", [P, NT, 6])
        mv1 = sb("mv1", [P, NT, 2])
        ve = sb("ve", [P, 4, NH * H1 + CW - H1])
        vp = sb("vp", [P, 2, NH, H1])
        carried = sb("carried", [P, NH, H1])
        hs = sb("hs", [P, 4, NH, H1])
        sq = sb("sq", [P, 2, NH, HD])
        qm = sb("qm", [P, 2, G, HG, P])
        xt = sb("xt", [P, 2, D])
        xtT = sb("xtT", [P, 2, G, P])
        base = sb("base", [P, 2, D])
        state = sb("state", [P, 2, G, HG * H1])
        fresh = sb("fresh", [P, G * HG * H1])
        tok = sb("tok", [P, 2, CH, P])
        chdec = sb("chdec", [P, B * G, 2])
        small = sb("small", [P, 6, 2, NH])
        st2 = sb("st2", [P, 2, 6])
        bcoef = sb("bcoef", [P, NT, 2])
        gsb = sb("gsb", [P, CH, 2, R])
        chsel = sb("chsel", [P, HB * G, 2])
        logits = sb("logits", [P, CH, E])
        lwork = sb("lwork", [P, 4, CH, E])
        hot = sb("hot", [P, B, CH, E], BF16)
        hotsum = sb("hotsum", [P, E], BF16)
        hotpart = sb("hotpart", [P, E], BF16)
        rsm = sb("rsm", [P, 8, CH])
        slot = sb("slot", [P, NT], U32)
        wg_in = sb("wg_in", [P, 3 * G, 2, NH])
        wg = sb("wg", [P, 2 * G, CW])
        wr = sb("wr", [P, G, CW])
        bias = sb("bias", [2 * R, 1])
        NC = consts.shape[1]
        cst = sb("cst", [P, NC])
        cstb = sb("cstb", [P, 2 * P], BF16)
        xinit = sb("xinit", [P, ROW])

        ident = cst[:, 0:P]
        o = P
        blockmask = cst[:, o:o + G * HG * H1]; o += G * HG * H1
        headrow = cst[:, o:o + P]; o += P
        bgmask = cst[:, o:o + B * G]; o += B * G
        rev = cst[:, o:o + E]; o += E
        tri_f = cst[:, o:o + 2 * P]; o += 2 * P
        neghalf = cst[:, o:o + 2 * NH]; o += 2 * NH
        assert o == NC and R == B * NH and S == 2 * D and CH == 4
        tri, ones = cstb[:, 0:P], cstb[:, P:2 * P]
        one_col = tri_f[:, P:P + 1]

        gates_sb, logf, cumf, a_row, m_row, neg_row = (
            Wflat[:, NSLOT - 2 + i // 3, (i % 3) * S:(i % 3 + 1) * S] for i in range(6))
        args = xt[:].rearrange("p n d -> p (n d)")
        m_seq = Wflat[:, NSLOT - 5:NSLOT - 2, :].rearrange("p s n -> p (s n)")[:, 0:CH * NH * P].rearrange(
            "p (h c i) -> p h c i", h=NH, c=CH)
        LATE = 5

        pool_f = qkT[:].rearrange("p a t -> p (a t)")
        NR = 16
        f = [0]

        def cut(n):
            f[0] += n
            return pool_f[:, f[0] - n:f[0]]

        erow = cut(NR * ROW).rearrange("p (e r) -> p e r", e=NR)
        ext = cut(2 * D).rearrange("p (e r) -> p e r", e=2)
        ebase = cut(4 * D).rearrange("p (e r) -> p e r", e=4)
        eout = cut(4 * D).rearrange("p (e r) -> p e r", e=4)
        extT = cut(2 * G * CW).rearrange("p (e g c) -> p e g c", e=2, g=G)
        esil = cut(2 * G * C).rearrange("p (e g c) -> p e g c", e=2, g=G)
        ehT = cut(2 * G * C).rearrange("p (e g c) -> p e g c", e=2, g=G)

        pq = psum("pq", [P, 4, 512])
        pown = psum("pown", [P, 512])
        pearly = psum("pearly", [P, 512])
        pstate = psum("pstate", [P, 512])
        pmisc = psum("pmisc", [P, 512])

        gate_bank, row_bank, tok_bank, dec_bank = (pown, pmisc), (pearly, pmisc), (pstate, pmisc), (pearly, pmisc)
        own = pown[:, 0:NH * H1]
        early = pearly[:, 0:NH * H1]

        def xtT_ps(n):
            return (pmisc if n <= NT - LAG else pq[:, n % 4])[:, 0:G * P]

        def log_ps(n):
            return (pmisc if n <= NT - LAG else pq[:, n % 4])[:, G * P:G * P + CW]

        cnt_ps = pmisc[:, 256 + CW:256 + CW + CH * E]

        x_in = [sem(f"x_in{i}") for i in range(len(LOADS))]
        c_in = [sem(f"c_in{i}") for i in range(len(LOADS))]
        cst_in, par_in, par_in2 = sem("cst_in"), sem("par_in"), sem("par_in2")
        w_in = [sem(f"w_in{s}") for s in range(NSLOT)]
        init_set, init_out = sem("init_set"), sem("init_out")
        cstb_set, ones_set = sem("cstb_set"), sem("ones_set")
        ln1_ready, xn_ready, tr1_ready, qk_copied = sem("ln1_ready"), sem("xn_ready"), sem("tr1_ready"), sem("qk_copied")
        rstd1_ready = sem("rstd1_ready")
        gates_done, gates_copied, gatesT_done, gatesT_copied = (
            sem("gates_done"), sem("gates_copied"), sem("gatesT_done"), sem("gatesT_copied"))
        softplus_ready, gate_step, args_ready, exps_ready = (
            sem("softplus_ready"), sem("gate_step"), sem("args_ready"), sem("exps_ready"))
        act_gate, stats1_ready, aggr1_ready = sem("act_gate"), sem("stats1_ready"), sem("aggr1_ready")
        m_ready, m_in = sem("m_ready"), [sem(f"m_in{b}") for b in range(B)]
        tokT_done, tok_ready, chsel_ready, chdec_done, chdec_ready = (
            sem("tokT_done"), sem("tok_ready"), sem("chsel_ready"), sem("chdec_done"), sem("chdec_ready"))
        mb_raw, mb_ready = sem("mb_raw"), sem("mb_ready")
        ve_ready, vp_ready = sem("ve_ready"), sem("vp_ready")
        scores_done, exp_done, c_ready = sem("scores_done"), sem("exp_done"), sem("c_ready")
        own_done, early_done, state_done, state_ready = (
            sem("own_done"), sem("early_done"), sem("state_done"), sem("state_ready"))
        fresh_ready, carried_ready, hs_ready = sem("fresh_ready"), sem("carried_ready"), sem("hs_ready")
        sq_ready, z_ready, r_ready = sem("sq_ready"), sem("z_ready"), sem("r_ready")
        scaled_ready = sem("scaled_ready")
        norm_step, var_ready, rstd_ready, xt_ready = (
            sem("norm_step"), sem("var_ready"), sem("rstd_ready"), sem("xt_ready"))
        base_ready = sem("base_ready")
        base_out = [sem(f"base_out{i}") for i in range(2)]
        xtT_done, xtT_ready, log_done, log_ready = sem("xtT_done"), sem("xtT_ready"), sem("log_done"), sem("log_ready")
        route_step, lexp_in, lexp_ready, hot_ready, cnt_done, slot_ready = (
            sem("route_step"), sem("lexp_in"), sem("lexp_ready"), sem("hot_ready"), sem("cnt_done"), sem("slot_ready"))
        cnt_read = sem("cnt_read")
        rows_out = sem("rows_out")
        erow_in = [sem(f"erow_in{i}") for i in range(4)]
        e_xt, e_xtT_done, e_xtT, e_base = sem("e_xt"), sem("e_xtT_done"), sem("e_xtT"), sem("e_base")
        e_gu, e_sil, e_h, e_y, e_out = sem("e_gu"), sem("e_sil"), sem("e_h"), sem("e_y"), sem("e_out")
        e_stored = [sem(f"e_stored{i}") for i in range(4)]
        idset, e_pad = sem("idset"), sem("e_pad")
        zeros_set, wg_ready = sem("zeros_set"), sem("wg_ready")
        qm_in = [sem(f"qm_in{i}") for i in range(2)]
        coef_ready = sem("coef_ready")

        block = stack.enter_context(nc.Block())

        def chunk(n):
            return slice(n * P, (n + 1) * P)

        PAIRS = NT // 2 - 1

        def first(u):
            return 2 * u if u <= PAIRS else PAIRS + u

        def chunks_of(u):
            return 2 if u < PAIRS else 1

        def unit_of(n):
            return n // 2 if n < 2 * PAIRS else n - PAIRS

        def halves(u):
            return slice(first(u) % 2, first(u) % 2 + chunks_of(u))

        def rows_of(u):
            return slice(first(u), first(u) + chunks_of(u))

        def sums_of(u):
            return slice(first(u) % 4, first(u) % 4 + chunks_of(u))

        def n_state(n):
            return (n // CH) * (CH - 1) + min(n % CH + 1, CH - 1)

        @block.sync
        def _(sp):
            for i, (a, z) in enumerate(LOADS):
                sp.dma_start(rowsX[:, a:z, 0:D], x_t[:, a:z, :]).then_inc(x_in[i], 16)
                if i == 0:
                    sp.dma_start(cst[:], consts).then_inc(cst_in, 16)
                sp.dma_start(ctxN[:, a:z, :], ctx_t[:, a:z, :]).then_inc(c_in[i], 16)
                if i == 0:
                    with nc.allow_non_contiguous_dma(reason="small parameters"):
                        for k, kern in enumerate((ik, fk)):
                            sp.dma_start(wg_in[:, :, k, :], kern.rearrange("(a p) h -> p a h", p=P)).then_inc(par_in, 16)
            with nc.allow_non_contiguous_dma(reason="small parameters"):
                sp.wait_ge(zeros_set, 1)
                sp.dma_start(wr[:, :, 0:E], w_router.rearrange("(g p) e -> p g e", p=P)).then_inc(par_in2, 16)
                for i, bb in enumerate((ib, fb)):
                    for r in range(B):
                        lo = (i * B + r) * NH
                        sp.dma_start(bias[lo:lo + NH, :], bb.rearrange("(h a) -> h a", a=1)).then_inc(par_in2, 16)

            def load_expert(e):
                s = e % NSLOT
                for m, w in enumerate((w_gate, w_up, w_down)):
                    sp.dma_start(W[:, s, m, :, :], w[e].rearrange("(p g) f -> p g f", g=G)).then_inc(w_in[s], 16)

            def store_base(n):
                sp.wait_ge(base_ready, n + 1)
                sp.dma_start(out_t[:, n, :], base[:, n % 2, :]).then_inc(base_out[n % 2], 16)

            def spread_queries(n):
                if n == 0:
                    sp.wait_ge(zeros_set, 2)
                sp.wait_ge(qk_copied, n + 1)
                if n >= 2:
                    sp.wait_ge(scores_done, n - 1)
                for h in range(HG):
                    r = slice(h * HD, (h + 1) * HD)
                    sp.dma_start(qm[r, n % 2, :, h, :], qT[r, :, chunk(n)]).then_inc(qm_in[n % 2], 16)

            spread_queries(0)
            spread_queries(1)

            def store_m(f):
                sp.wait_ge(m_ready, f + 1)
                for b in range(f * HB, (f + 1) * HB):
                    r = b % HB * NH
                    sp.dma_start(m_seq[32 * b:32 * b + 1].rearrange("p h c i -> p h (c i)"),
                                 neg_row[r:r + NH, :]).then_inc(m_in[b], 16)

            store_m(0)
            for n in range(2, NT):
                spread_queries(n)
                if n - 2 < NSLOT - LATE:
                    load_expert(n - 2)
                if n == 4:
                    sp.wait_ge(init_set, 2)
                    k = SLOTS // P
                    sp.dma_start(xbuf.rearrange("(p k) r -> p k r", k=k),
                                 xinit[:].unsqueeze(1).broadcast_to([P, k, ROW])).then_inc(init_out, 16)
                    store_m(1)
                if n >= 7:
                    store_base(n - 7)
            sp.wait_ge(mb_raw, NT)
            sp.wait_ge(exps_ready, 2)
            for e in range(NSLOT - LATE, NSLOT):
                load_expert(e)
            for n in range(NT - 7, NT):
                store_base(n)

            def load_rows(q):
                sp.dma_start(erow[0:C, 4 * q % NR:4 * q % NR + 4, :],
                             xbuf[4 * q * C:4 * (q + 1) * C, :].rearrange("(e c) r -> c e r", c=C)
                             ).then_inc(erow_in[q % 4], 16)

            sp.wait_ge(rows_out, 16 * NT)
            for q in range(NR // 4):
                load_rows(q)
            for e in range(E):
                if e % 4 == 3 and e // 4 + NR // 4 < E // 4:
                    for i in range(4):
                        sp.wait_ge(e_stored[i], 16 * (e // 4 + 1))
                    load_rows(e // 4 + NR // 4)
                if e + NSLOT < E:
                    sp.wait_ge(e_y, e + 1)
                    load_expert(e + NSLOT)
            for i in range(4):
                sp.wait_ge(e_stored[i], 16 * (E // 4))

        @block.gpsimd
        def _(pool):
            nc.gpsimd.memset(xinit[:], 0.0).then_inc(init_set, 1)
            pool.wait_ge(init_set, 1)
            nc.gpsimd.iota(xinit[:, D + 3:D + 4].bitcast(I32), pattern=[[0, 1]], base=T,
                           channel_multiplier=0).then_inc(init_set, 1)
            nc.gpsimd.iota(rowsX[:, :, D + 3].bitcast(I32), pattern=[[P, NT]], base=0,
                           channel_multiplier=1).then_inc(idset, 1)
            nc.gpsimd.memset(wr[:], 0.0).then_inc(zeros_set, 1)
            nc.gpsimd.memset(ve[:], 1.0).then_inc(ones_set, 1)
            nc.gpsimd.memset(qm[:], 0.0).then_inc(zeros_set, 1)
            pool.wait_ge(cst_in, 16)
            for i, (a, z) in enumerate(LOADS):
                pool.wait_ge(ln1_ready, i + 1)
                v = mv1[:, a:z, 1]
                nc.gpsimd.tensor_tensor(v, v, neghalf[:, 0:z - a], ALU.pow).then_inc(rstd1_ready, 1)

            def broadcast_m(n, s):
                b, c = divmod(n, CH)
                pool.wait_ge(m_in[b], 16)
                if n == 4:
                    pool.wait_ge(tr1_ready, NT)
                if n >= 5:
                    pool.wait_ge(own_done, n - 4)
                for signal, count in ((mb_ready, n),
                                      (r_ready, (s - 1) // 2), (rstd_ready, (s - 2) // 2)):
                    if count > 0:
                        pool.wait_ge(signal, count)
                v = decay[:, n % 5, :].rearrange("p (h i) -> p h i", i=P)
                nc.gpsimd.partition_broadcast(v, m_seq[32 * b:32 * b + 1, :, c, :], channels=P).then_inc(mb_raw, 1)
                pool.wait_ge(mb_raw, n + 1)
                nc.gpsimd.affine_select(out=v, in_=v, compare_op=ALU.is_ge, fill=NEG, base=0,
                                        pattern=[[0, NH], [1, P]], channel_multiplier=-1).then_inc(mb_ready, 1)

            pool.wait_ge(ones_set, 1)
            pool.wait_ge(zeros_set, 2)
            broadcast_m(0, 0)
            broadcast_m(1, 0)
            broadcast_m(2, 0)

            def scatter_rows(b):
                pool.wait_ge(slot_ready, b + 1)
                if b == 0:
                    pool.wait_ge(init_out, 16)
                    pool.wait_ge(idset, 1)
                for n in range(b * CH, (b + 1) * CH):
                    nc.gpsimd.indirect_dma_start(
                        out=xbuf, out_offset=bass.IndirectOffsetOnAxis(ap=slot[:, n:n + 1], axis=0),
                        in_=rowsX[:, n, :], in_offset=None, bounds_check=SLOTS - 1,
                        oob_is_err=False).then_inc(rows_out, 16)

            def head_scale(u):
                pool.wait_ge(z_ready, u + 1)
                nc.gpsimd.tensor_tensor(small[:, 4 + u % 2, halves(u)].rearrange("p c h -> p (c h)"),
                                        small[:, 2 + u % 2, halves(u)].rearrange("p c h -> p (c h)"),
                                        neghalf[:, 0:NH * chunks_of(u)], ALU.pow).then_inc(r_ready, 1)

            def row_scale(u):
                pool.wait_ge(var_ready, u + 1)
                v = rowsX[:, rows_of(u), D + 1]
                nc.gpsimd.tensor_tensor(v, v, neghalf[:, 0:chunks_of(u)], ALU.pow).then_inc(rstd_ready, 1)

            for s in range(NT):
                if s + 3 < NT:
                    broadcast_m(s + 3, s)
                elif s >= NT - 2:
                    scatter_rows(s - NT + 2)
                if s % 2 == 0 and s >= 2:
                    head_scale((s - 2) // 2)
                if s % 2 == 1 and s >= 3:
                    row_scale((s - 3) // 2)
            for u in (PAIRS, PAIRS + 1):
                head_scale(u)
            for u in (PAIRS, PAIRS + 1):
                row_scale(u)
            scatter_rows(B - 2)
            scatter_rows(B - 1)
            for e in range(E + 2):
                if e < E:
                    pool.wait_ge(e_xt, e + 1)
                    if e >= 4:
                        pool.wait_ge(e_out, e - 3)
                    nc.gpsimd.tensor_tensor(ebase[0:C, e % 4, :], erow[0:C, e % NR, 0:D], ext[0:C, e % 2, :],
                                            ALU.add).then_inc(e_base, 1)
                d = e - 2
                if d == 0:
                    for i in range(2):
                        pool.wait_ge(base_out[i], 16 * NT // 2)
                if d >= 0:
                    pool.wait_ge(e_out, d + 1)
                    nc.gpsimd.indirect_dma_start(
                        out=out_rows, out_offset=bass.IndirectOffsetOnAxis(
                            ap=erow[0:C, d % NR, D + 3:D + 4].bitcast(U32), axis=0),
                        in_=eout[0:C, d % 4, :], in_offset=None, bounds_check=T - 1,
                        oob_is_err=False).then_inc(e_stored[d % 4], 16)

        @block.scalar
        def _(act):
            def copy_qk(n):
                act.wait_ge(tr1_ready, n + 1)
                nc.scalar.copy(qkT[:, :, chunk(n)],
                               pq[:, n % 4, :].rearrange("p (a t) -> p a t", t=P)).then_inc(qk_copied, 1)

            def softplus_exp(f):
                act.wait_ge(gatesT_done, f + 1)
                if f == 0:
                    act.wait_ge(par_in2, 16 * (1 + 2 * B))
                else:
                    act.wait_ge(args_ready, 2)
                nc.scalar.activation(logf[0:R, :], row_bank[f][R:2 * R, :], ACT.Abs,
                                     bias=bias[R:2 * R, 0:1]).then_inc(act_gate, 1)
                act.wait_ge(act_gate, 2 * f + 1)
                nc.scalar.activation(logf[0:R, :], logf[0:R, :], ACT.Exp, scale=-1.0).then_inc(act_gate, 1)

            def softplus_ln(f):
                act.wait_ge(act_gate, 2 * f + 2)
                nc.scalar.activation(logf[0:R, :], logf[0:R, :], ACT.Ln, bias=1.0).then_inc(softplus_ready, 1)

            def exp_args(f):
                act.wait_ge(args_ready, 2 * f + 1)
                nc.scalar.activation(args[0:3 * R, :], args[0:3 * R, :], ACT.Exp).then_inc(exps_ready, 1)

            def copy_tok(f):
                act.wait_ge(tokT_done, f + 1)
                nc.scalar.copy(tok[:, f], tok_bank[f][:].rearrange("p (c r) -> p c r", c=CH)).then_inc(tok_ready, 1)

            for n in range(NT):
                copy_qk(n)
                if n == HN + 1:
                    softplus_exp(0)
                if n == HN + 2:
                    softplus_ln(0)
            exp_args(0)
            copy_tok(0)
            act.wait_ge(tok_ready, 1)

            def values(n):
                if n in LOAD_AT:
                    act.wait_ge(c_in[LOAD_AT[n]], 16)
                if n >= 4:
                    act.wait_ge(own_done, n - 3)
                    act.wait_ge(vp_ready, n_state(n - 4))
                nc.scalar.copy(ve[:, n % 4, 0:NH * H1].rearrange("p (h d) -> p h d", h=NH)[:, :, 0:HD],
                               ctxN[:, n, :].rearrange("p (h d) -> p h d", h=NH)).then_inc(ve_ready, 1)

            def decay_of(n):
                b, c = divmod(n, CH)
                if n == HN:
                    act.wait_ge(tok_ready, 2)
                f, r0 = n // HN, 3 * R + b % HB * NH
                act.wait_ge(mb_ready, n + 1)
                for h in range(NH):
                    v = decay[:, n % 5, h * P:(h + 1) * P]
                    last = nc.scalar.activation(v, v, ACT.Exp,
                                                bias=tok[:, f, c, r0 + h:r0 + h + 1])
                last.then_inc(exp_done, 1)

            def squares(u):
                act.wait_ge(hs_ready, first(u) + chunks_of(u))
                if 1 <= u <= PAIRS:
                    act.wait_ge(z_ready, u)
                nc.scalar.activation(sq[:, halves(u)], hs[:, sums_of(u), :, 0:HD], ACT.Square,
                                     scale=float(HD) ** -0.5).then_inc(sq_ready, 1)

            def norm_x1(n):
                act.wait_ge(coef_ready, unit_of(n) + 1)
                if n == 0:
                    act.wait_ge(chsel_ready, 2)
                if n >= 2:
                    act.wait_ge(xtT_done, n - 1)
                nc.scalar.activation(xt[:, n % 2, :], rowsX[:, n, 0:D], ACT.Identity, bias=bcoef[:, n, 1:2],
                                     scale=rowsX[:, n, D + 1:D + 2]).then_inc(xt_ready, 1)

            def copy_x1(n):
                act.wait_ge(xtT_done, n + 1)
                if n >= 2:
                    act.wait_ge(log_done, n - 1)
                nc.scalar.copy(xtT[:, n % 2], xtT_ps(n).rearrange("p (g t) -> p g t", g=G)).then_inc(xtT_ready, 1)

            def base_rows(n):
                act.wait_ge(coef_ready, unit_of(n) + 1)
                if n >= 2:
                    act.wait_ge(base_out[n % 2], 16 * (n // 2))
                nc.scalar.activation(base[:, n % 2, :], rowsX[:, n, 0:D], ACT.Identity,
                                     bias=bcoef[:, n, 1:2], scale=bcoef[:, n, 0:1]).then_inc(base_ready, 1)

            def copy_logits(n):
                act.wait_ge(log_done, n + 1)
                if n >= CH and n % CH == 0:
                    act.wait_ge(hot_ready, n // CH)
                nc.scalar.copy(logits[:, n % CH, :], log_ps(n)[:, 0:E]).then_inc(log_ready, 1)

            def exp_logits(b):
                act.wait_ge(lexp_in, b + 1)
                nc.scalar.activation(lwork[:, 1], lwork[:, 0], ACT.Exp).then_inc(lexp_ready, 1)

            act.wait_ge(ones_set, 1)
            values(0)
            values(1)
            decay_of(0)
            softplus_exp(1)
            for s in range(NT):
                if s + 1 < NT:
                    decay_of(s + 1)
                if s == 0:
                    softplus_ln(1)
                if s == 3:
                    exp_args(1)
                if s == 4:
                    copy_tok(1)
                if s + 2 < NT:
                    values(s + 2)
                if s >= LAG:
                    norm_x1(s - LAG)
                if s >= LAG + 1:
                    copy_logits(s - LAG - 1)
                if s >= CHOSEN and (s - CHOSEN) % CH == 0:
                    exp_logits((s - CHOSEN) // CH)
                if s >= LAG:
                    copy_x1(s - LAG)
                if s % 2 == 0 and s >= 2:
                    squares((s - 2) // 2)
                if s == NT - 1:
                    squares(PAIRS)
                if s >= LAG:
                    base_rows(s - LAG)
            n = NT - LAG
            norm_x1(n)
            copy_logits(n - 1)
            copy_x1(n)
            squares(PAIRS + 1)
            copy_logits(n)
            norm_x1(n + 1)
            norm_x1(n + 2)
            copy_x1(n + 1)
            copy_x1(n + 2)
            norm_x1(n + 3)
            norm_x1(n + 4)
            copy_x1(n + 3)
            exp_logits(B - 2)
            copy_x1(n + 4)
            for i in range(1, LAG):
                copy_logits(n + i)
            base_rows(n)
            base_rows(n + 1)
            exp_logits(B - 1)
            for i in range(2, LAG):
                base_rows(n + i)
            for e in range(E):
                act.wait_ge(e_gu, e + 1)
                if e >= 2:
                    act.wait_ge(e_h, e - 1)
                nc.scalar.activation(esil[:, e % 2],
                                     pq[:, e % 2, 0:G * CW].rearrange("p (g c) -> p g c", g=G)[:, :, 0:C],
                                     ACT.Silu).then_inc(e_sil, 1)

        @block.tensor
        def _(pe):
            def gates(n):
                pe.wait_ge(qk_copied, n + 1)
                for i in range(2 * G):
                    o_ = gate_bank[n // HN][:, n % HN * 2 * NH:n % HN * 2 * NH + CW]
                    last = nc.tensor.matmul(o_, qkT[:, i, chunk(n)], wg[:, i, :],
                                            start=(i == 0), stop=(i == 2 * G - 1))
                last.then_inc(gates_done, 1)

            def gate_rows(f):
                pe.wait_ge(gates_copied, f + 1)
                for c in range(CH):
                    last = nc.tensor.transpose(row_bank[f][0:2 * R, chunk(c)],
                                               gsb[:, c].rearrange("p g r -> p (g r)"), ident)
                last.then_inc(gatesT_done, 1)

            def token_gates(f):
                pe.wait_ge(exps_ready, f + 1)
                pe.wait_ge(args_ready, 2 * f + 2)
                if f == 1:
                    pe.wait_ge(gatesT_copied, 2)
                for c in range(CH):
                    last = nc.tensor.transpose(tok_bank[f][:, chunk(c)], args[:, chunk(c)], ident)
                last.then_inc(tokT_done, 1)

            def state_decays(f):
                pe.wait_ge(chsel_ready, f + 1)
                if f == 0:
                    pe.wait_ge(gatesT_copied, 1)
                else:
                    pe.wait_ge(tok_ready, 2)
                nc.tensor.matmul(dec_bank[f][:, 0:2 * HB * G], headrow[R:2 * R, :],
                                 chsel[R:2 * R].rearrange("p g k -> p (g k)"), start=True,
                                 stop=True).then_inc(chdec_done, 1)

            pe.wait_ge(cst_in, 16)
            for n in range(NT):
                if n in LOAD_AT:
                    pe.wait_ge(c_in[LOAD_AT[n]], 16)
                pe.wait_ge(xn_ready, n + 1)
                if n >= 4:
                    pe.wait_ge(qk_copied, n - 3)
                for i in range(2 * G):
                    src = xn[:, n % 4, i * P:(i + 1) * P] if i < G else ctxN[:, n, (i - G) * P:(i - G + 1) * P]
                    last = nc.tensor.transpose(pq[:, n % 4, i * P:(i + 1) * P], src, ident)
                last.then_inc(tr1_ready, 1)
                if n == 1:
                    pe.wait_ge(wg_ready, 3)
                if n >= 1:
                    gates(n - 1)
                if n == HN + 1:
                    gate_rows(0)

            def scores(n):
                pe.wait_ge(qm_in[n % 2], 16 * HG * (n // 2 + 1))
                if n >= 2:
                    pe.wait_ge(c_ready, n - 1)
                for g in range(G):
                    last = nc.tensor.matmul(pq[:, 2 * (n % 2) + g, :], kT[:, g, chunk(n)],
                                            qm[:, n % 2, g].rearrange("p h i -> p (h i)"), start=True, stop=True)
                last.then_inc(scores_done, 1)

            scores(0)
            token_gates(0)
            state_decays(0)
            gates(NT - 1)
            gate_rows(1)

            def outputs(n):
                c = n % CH
                if c > 0:
                    pe.wait_ge(state_ready, n_state(n - 1))
                    if n == 1:
                        pe.wait_ge(chdec_ready, 1)
                    if n_state(n - 1) > 1:
                        pe.wait_ge(carried_ready, n_state(n - 1) - 1)
                    for g in range(G):
                        w = HG * H1
                        last = nc.tensor.matmul(early[:, g * w:(g + 1) * w], qT[:, g, chunk(n)],
                                                state[:, n_state(n - 1) % 2, g, :], start=True, stop=True)
                    last.then_inc(early_done, 1)
                pe.wait_ge(c_ready, n + 1)
                pe.wait_ge(ve_ready, n + 1)
                if n == 0:
                    pe.wait_ge(gates_copied, 1)
                else:
                    pe.wait_ge(hs_ready, n)
                for h in range(NH):
                    last = nc.tensor.matmul(pown[:, h * H1:h * H1 + CW], decay[:, n % 5, h * P:(h + 1) * P],
                                            ve[:, n % 4, h * H1:h * H1 + CW], start=True, stop=True)
                last.then_inc(own_done, 1)

            def state_sum(n):
                k = n_state(n)
                pe.wait_ge(vp_ready, k)
                if k > 1:
                    pe.wait_ge(fresh_ready, k - 1)
                else:
                    pe.wait_ge(tok_ready, 1)
                w = HG * H1
                for g in range(G):
                    last = nc.tensor.matmul(pstate[:, g * w:(g + 1) * w], ctxN[:, n, g * P:(g + 1) * P],
                                            vp[:, k % 2, g * HG:(g + 1) * HG, :].rearrange("p h d -> p (h d)"),
                                            start=True, stop=True)
                last.then_inc(state_done, 1)

            def router(n):
                pe.wait_ge(xtT_ready, n + 1)
                if n == 0:
                    pe.wait_ge(par_in2, 16 * (1 + 2 * B))
                for g in range(G):
                    last = nc.tensor.matmul(log_ps(n), xtT[:, n % 2, g, :], wr[:, g, :], start=(g == 0),
                                            stop=(g == G - 1))
                last.then_inc(log_done, 1)

            def counts(b):
                pe.wait_ge(hot_ready, b + 1)
                for t in range(CH):
                    o_ = cnt_ps[:, t * E:(t + 1) * E]
                    nc.tensor.matmul(o_, ones, hotsum[:], start=True, stop=False)
                    for u in range(t):
                        nc.tensor.matmul(o_, ones, hot[:, b, u, :], start=False, stop=False)
                    last = nc.tensor.matmul(o_, tri, hot[:, b, t, :], start=False, stop=True)
                last.then_inc(cnt_done, 1)

            def transpose_x1(n):
                pe.wait_ge(xt_ready, n + 1)
                if n == 0:
                    pe.wait_ge(chdec_ready, 2)
                for g in range(G):
                    last = nc.tensor.transpose(xtT_ps(n)[:, g * P:(g + 1) * P], xt[:, n % 2, g * P:(g + 1) * P], ident)
                last.then_inc(xtT_done, 1)

            for s in range(NT):
                if s >= 1:
                    scores(s)
                if s % CH < CH - 1:
                    state_sum(s)
                if s >= LAG + 1:
                    if s > CHOSEN:
                        pe.wait_ge(cnt_read, (s - CHOSEN - 1) // CH + 1)
                    router(s - LAG - 1)
                if s >= 1:
                    outputs(s - 1)
                if s >= LAG:
                    if s > LAG:
                        pe.wait_ge(log_ready, s - LAG)
                    transpose_x1(s - LAG)
                if s == 3:
                    token_gates(1)
                if s == 4:
                    state_decays(1)
                if s >= CHOSEN and (s - CHOSEN) % CH == 0:
                    pe.wait_ge(xtT_ready, s - LAG + 1)
                    counts((s - CHOSEN) // CH)
            n = NT - LAG
            pe.wait_ge(cnt_read, B - 2)
            router(n - 1)
            outputs(NT - 1)
            pe.wait_ge(log_ready, n)
            transpose_x1(n)
            router(n)
            pe.wait_ge(c_ready, NT)
            transpose_x1(n + 1)
            transpose_x1(n + 2)
            router(n + 1)
            router(n + 2)
            transpose_x1(n + 3)
            router(n + 3)
            pe.wait_ge(log_ready, n + 1)
            counts(B - 2)
            transpose_x1(n + 4)
            router(n + 4)
            pe.wait_ge(cnt_read, B - 1)
            counts(B - 1)

            def e_transpose(e):
                pe.wait_ge(e_xt, e + 1)
                if e >= 2:
                    pe.wait_ge(e_xtT, e - 1)
                bank = (pown, pearly)[e % 2]
                v = ext[0:C, e % 2, :].rearrange("c (p g) -> c g p", g=G)
                for g in range(G):
                    last = nc.tensor.transpose(bank[:, g * C:(g + 1) * C], v[:, g, :], ident[0:C, 0:C])
                last.then_inc(e_xtT_done, 1)

            def e_gate_up(e):
                s = e % NSLOT
                pe.wait_ge(w_in[s], 48 * (e // NSLOT + 1))
                pe.wait_ge(e_pad, 1)
                pe.wait_ge(e_xtT, e + 1)
                if e >= 2:
                    pe.wait_ge(e_h, e - 1)
                for m in range(2):
                    for j in range(G):
                        o_ = pq[:, e % 2, (m * G + j) * CW:(m * G + j + 1) * CW]
                        for g in range(G):
                            w = W[:, s, m, g, :].rearrange("p (m j) -> p j m", j=G)[:, j, :]
                            last = nc.tensor.matmul(o_, w, extT[:, e % 2, g, :], start=(g == 0), stop=(g == G - 1))
                last.then_inc(e_gu, 1)

            def e_down(e):
                pe.wait_ge(e_h, e + 1)
                if e >= 2:
                    pe.wait_ge(e_out, e - 1)
                for j in range(G):
                    last = nc.tensor.matmul(pq[0:C, 2 + e % 2, 0:D], ehT[:, e % 2, j, :], W[:, e % NSLOT, 2, j, :],
                                            start=(j == 0), stop=(j == G - 1))
                last.then_inc(e_y, 1)

            pe.wait_ge(slot_ready, B)
            pe.wait_ge(fresh_ready, n_state(NT - 1))
            for _ in range(28):
                nc.tensor.matmul(pstate[:, 0:P], ident, ident, start=True, stop=True)
            e_transpose(0)
            for e in range(E):
                if e + 1 < E:
                    e_transpose(e + 1)
                e_gate_up(e)
                if e >= 1:
                    e_down(e - 1)
            e_down(E - 1)

        @block.vector
        def _(dve):
            V = nc.vector
            V.memset(wg[:], 0.0).then_inc(wg_ready, 1)
            V.memset(hotsum[:], 0.0).then_inc(cstb_set, 1)
            V.memset(gsb[:], 0.0).then_inc(cstb_set, 1)

            def norm_x(n):
                if n in LOAD_AT:
                    dve.wait_ge(rstd1_ready, LOAD_AT[n] + 1)
                if n >= 4:
                    dve.wait_ge(tr1_ready, n - 3)
                V.tensor_scalar(xn[:, n % 4, :], rowsX[:, n, 0:D], mv1[:, n, 0:1], mv1[:, n, 1:2],
                                ALU.subtract, ALU.mult).then_inc(xn_ready, 1)

            def stats_x(i):
                a, z = LOADS[i]
                dve.wait_ge(x_in[i], 16)
                for n in range(a, z):
                    V.bn_stats(st1[:, n, :], rowsX[:, n, 0:D]).then_inc(stats1_ready, 1)
                for n in range(a, z):
                    dve.wait_ge(stats1_ready, n + 1)
                    V.bn_aggr(mv1[:, n, :], st1[:, n, :]).then_inc(aggr1_ready, 1)
                dve.wait_ge(aggr1_ready, z)
                v = mv1[:, a:z, 1]
                V.tensor_scalar(v, v, LN_EPS, None, ALU.add).then_inc(ln1_ready, 1)

            gs = [0]

            def step(ins):
                gs[0] += 1
                ins.then_inc(gate_step, 1)
                dve.wait_ge(gate_step, gs[0])

            def copy_gates(f):
                dve.wait_ge(gates_done, (f + 1) * HN)
                if f == 0:
                    dve.wait_ge(cstb_set, 2)
                else:
                    dve.wait_ge(gatesT_done, 1)
                pgate = gate_bank[f][:, 0:HN * 2 * NH].rearrange("p (b c g h) -> p c g b h", b=HB, c=CH, g=2)
                for c in range(CH):
                    last = V.tensor_copy(gsb[:, c, :, 0:RH].rearrange("p g (b h) -> p g b h", b=HB), pgate[:, c])
                last.then_inc(gates_copied, 1)

            def add_bias(f):
                dve.wait_ge(act_gate, 2 * f + 1)
                dve.wait_ge(gatesT_done, f + 1)
                dve.wait_ge(par_in2, 16 * (1 + 2 * B))
                V.tensor_scalar(gates_sb[0:2 * R, :], row_bank[f][0:2 * R, :], bias[:, 0:1], None,
                                ALU.add).then_inc(gatesT_copied, 1)
                dve.wait_ge(gatesT_copied, f + 1)
                step(V.tensor_scalar(cumf[0:R, :], gates_sb[R:2 * R, :], 0.0, None, ALU.min))

            def sum_log_forget(f):
                dve.wait_ge(softplus_ready, f + 1)
                step(V.tensor_tensor(logf[0:R, :], cumf[0:R, :], logf[0:R, :], ALU.subtract))
                step(V.tensor_tensor_scan(cumf[0:R, :], one_col[0:R, :].broadcast_to([R, S]), logf[0:R, :], 0.0,
                                          ALU.mult, ALU.add))

            def running_max(f):
                step(V.tensor_tensor(a_row[0:R, :], gates_sb[0:R, :], cumf[0:R, :], ALU.subtract))
                step(V.tensor_tensor_scan(m_row[0:R, :], a_row[0:R, :], a_row[0:R, :], -3.0e38, ALU.max, ALU.max))
                if f == 1:
                    for b in range(HB):
                        dve.wait_ge(m_in[b], 16)
                V.tensor_scalar(neg_row[0:R, :], m_row[0:R, :], -1.0, None, ALU.mult).then_inc(m_ready, 1)

            A = args.rearrange("p (c i) -> p c i", c=CH)

            def exp_arguments(f):
                if f == 1:
                    dve.wait_ge(tokT_done, 1)
                mr = m_row[0:R, :].rearrange("p (c i) -> p c i", c=CH)
                ar = a_row[0:R, :].rearrange("p (c i) -> p c i", c=CH)
                ends = mr[:, :, P - 1:P].broadcast_to([R, CH, P])
                V.tensor_tensor(A[0:R], ar, ends, ALU.subtract)
                V.memset(A[R:2 * R, 0, :], 0.0)
                V.tensor_tensor(A[R:2 * R, 1:CH, :], mr[:, 0:CH - 1, P - 1:P].broadcast_to([R, CH - 1, P]),
                                mr[:, 1:CH, :], ALU.subtract)
                V.scalar_tensor_tensor(out=args[2 * R:3 * R, :], in0=cumf[0:R, :], scalar=-1.0, in1=m_row[0:R, :],
                                       op0=ALU.mult, op1=ALU.subtract).then_inc(args_ready, 1)
                V.tensor_copy(args[3 * R:4 * R, :], a_row[0:R, :]).then_inc(args_ready, 1)

            def select_decays(f):
                dve.wait_ge(exps_ready, f + 1)
                if f == 1:
                    dve.wait_ge(chdec_done, 1)
                V.tensor_tensor(chsel[R:2 * R], bgmask[R:2 * R, 0:HB * G].unsqueeze(2).broadcast_to([R, HB * G, 2]),
                                A[R:2 * R, 1:3, P - 1:P].rearrange("p a b -> p b a").broadcast_to([R, HB * G, 2]),
                                ALU.mult).then_inc(chsel_ready, 1)

            def copy_decays(f):
                dve.wait_ge(chdec_done, f + 1)
                V.tensor_copy(chdec[:, f * HB * G:(f + 1) * HB * G],
                              dec_bank[f][:, 0:2 * HB * G].rearrange("p (g k) -> p g k", k=2)).then_inc(chdec_ready, 1)

            stats_x(0)
            norm_x(0)
            norm_x(1)
            stats_x(1)
            dve.wait_ge(wg_ready, 1)
            dve.wait_ge(par_in, 16 * 2)
            wgs = wg[:, :, 0:2 * NH].rearrange("p a (i h) -> p a i h", i=2)
            V.tensor_copy(wgs[:, 0:G], wg_in[:, 0:G]).then_inc(wg_ready, 1)
            V.tensor_tensor(wgs[:, G:2 * G], wg_in[:, G:2 * G], wg_in[:, 2 * G:3 * G], ALU.add).then_inc(wg_ready, 1)
            dve.wait_ge(cst_in, 16)
            V.tensor_copy(cstb[:], tri_f).then_inc(cstb_set, 1)
            norm_x(2)
            norm_x(3)
            stats_x(2)
            for n in range(CH, 2 * CH):
                norm_x(n)
                if n == CH + 1:
                    stats_x(3)
            norm_x(HN)
            stats_x(4)
            norm_x(HN + 1)
            norm_x(HN + 2)
            norm_x(HN + 3)
            copy_gates(0)
            norm_x(HN + 4)
            add_bias(0)
            norm_x(HN + 5)
            sum_log_forget(0)
            norm_x(HN + 6)
            running_max(0)
            norm_x(HN + 7)
            exp_arguments(0)
            select_decays(0)
            copy_gates(1)
            copy_decays(0)
            dve.wait_ge(tok_ready, 1)
            dve.wait_ge(chdec_ready, 1)

            def decay_scores(n):
                dve.wait_ge(scores_done, n + 1)
                dve.wait_ge(exp_done, n + 1)
                V.scalar_tensor_tensor(out=decay[:, n % 5, :],
                                       in0=pq[:, 2 * (n % 2):2 * (n % 2) + 2, :].rearrange("p g i -> p (g i)"),
                                       scalar=float(HD) ** -0.5, in1=decay[:, n % 5, :],
                                       op0=ALU.mult, op1=ALU.mult).then_inc(c_ready, 1)

            def combine(n):
                b, c = divmod(n, CH)
                if n >= 4:
                    dve.wait_ge(norm_step, n // 2 - 1)
                ow = own.rearrange("p (h d) -> p h d", h=NH)
                if c > 0:
                    w = tok[:, b // HB, c, R + b % HB * NH:R + (b % HB + 1) * NH].unsqueeze(2).broadcast_to([P, NH, H1])
                    dve.wait_ge(early_done, n_state(n - 1))
                    V.tensor_tensor(carried[:], early.rearrange("p (h d) -> p h d", h=NH), w,
                                    ALU.mult).then_inc(carried_ready, 1)
                    dve.wait_ge(carried_ready, n_state(n - 1))
                    dve.wait_ge(own_done, n + 1)
                    V.tensor_tensor(hs[:, n % 4], ow, carried[:], ALU.add).then_inc(hs_ready, 1)
                else:
                    dve.wait_ge(own_done, n + 1)
                    V.tensor_copy(hs[:, n % 4], ow).then_inc(hs_ready, 1)

            def normalizer(u):
                b, c = divmod(first(u), CH)
                dve.wait_ge(hs_ready, first(u) + chunks_of(u))
                total = hs[:, sums_of(u), :, HD]
                n0, mean_sq = small[:, 0, halves(u)], small[:, 1, halves(u)]
                link(V.scalar_tensor_tensor(out=n0, in0=total, scalar=-1.0, in1=total, op0=ALU.mult, op1=ALU.max))
                link(V.tensor_tensor(n0, n0, tok[:, b // HB, c:c + chunks_of(u), 2 * R + b % HB * NH:2 * R + (b % HB + 1) * NH],
                                     ALU.max))
                link(V.tensor_scalar(n0, n0, NORM_EPS, None, ALU.add))
                link(V.tensor_tensor(n0, n0, n0, ALU.mult))
                dve.wait_ge(sq_ready, u + 1)
                link(V.tensor_reduce(mean_sq, sq[:, halves(u)], AX_X, ALU.add))
                if u >= 2:
                    dve.wait_ge(r_ready, u - 1)
                V.scalar_tensor_tensor(out=small[:, 2 + u % 2, halves(u)], in0=n0, scalar=1e-6, in1=mean_sq,
                                       op0=ALU.mult, op1=ALU.add).then_inc(z_ready, 1)

            links = [0]

            def link(ins):
                links[0] += 1
                ins.then_inc(route_step, 1)
                dve.wait_ge(route_step, links[0])

            def scaled_values(n):
                b, c = divmod(n, CH)
                dve.wait_ge(ve_ready, n + 1)
                if n_state(n) > 2:
                    dve.wait_ge(state_done, n_state(n) - 2)
                w = tok[:, b // HB, c, b % HB * NH:(b % HB + 1) * NH].unsqueeze(2).broadcast_to([P, NH, H1])
                V.tensor_tensor(vp[:, n_state(n) % 2],
                                        ve[:, n % 4, 0:NH * H1].rearrange("p (h d) -> p h d", h=NH), w,
                                        ALU.mult).then_inc(vp_ready, 1)

            def update_state(n):
                k = n_state(n)
                b, c = divmod(n, CH)
                dve.wait_ge(state_done, k)
                if k > 1:
                    dve.wait_ge(state_ready, k - 1)
                if c == 0:
                    if k > 1:
                        dve.wait_ge(early_done, k - 1)
                    V.tensor_tensor(state[:, k % 2].rearrange("p g w -> p (g w)"), pstate[:, 0:G * HG * H1],
                                    blockmask, ALU.mult).then_inc(fresh_ready, 1)
                    dve.wait_ge(fresh_ready, k)
                    V.engine_nop().then_inc(state_ready, 1)
                    return
                V.tensor_tensor(fresh[:], pstate[:, 0:G * HG * H1], blockmask, ALU.mult).then_inc(fresh_ready, 1)
                dve.wait_ge(fresh_ready, k)
                dve.wait_ge(early_done, max(1, k - 2))
                w = HG * H1
                for g in range(G):
                    last = V.scalar_tensor_tensor(out=state[:, k % 2, g, :], in0=state[:, (k - 1) % 2, g, :],
                                                  scalar=chdec[:, b * G + g, c - 1:c], in1=fresh[:, g * w:(g + 1) * w],
                                                  op0=ALU.mult, op1=ALU.add)
                last.then_inc(state_ready, 1)

            def residual(u):
                dve.wait_ge(r_ready, u + 1)
                hv = hs[:, sums_of(u)].rearrange("p c h d -> p (c h) d")[:, :, 0:HD]
                rs = small[:, 4 + u % 2, halves(u)].rearrange("p c h -> p (c h)")
                V.tensor_tensor(hv, hv, rs.unsqueeze(2).broadcast_to([P, NH * chunks_of(u), HD]),
                                ALU.mult).then_inc(scaled_ready, 1)
                dve.wait_ge(scaled_ready, u + 1)
                x3 = rowsX[:, rows_of(u), 0:D].rearrange("p c (h d) -> p c h d", h=NH)
                V.tensor_tensor(x3, x3, hs[:, sums_of(u), :, 0:HD], ALU.add).then_inc(norm_step, 1)
                dve.wait_ge(norm_step, u + 1)
                ns = range(first(u), first(u) + chunks_of(u))
                for n in ns:
                    last = V.bn_stats(st2[:, n % 2, :], rowsX[:, n, 0:D])
                link(last)
                for n in ns:
                    last = V.bn_aggr(rowsX[:, n, D:D + 2], st2[:, n % 2, :])
                link(last)
                v = rowsX[:, rows_of(u), D + 1]
                V.tensor_scalar(v, v, LN_EPS, None, ALU.add).then_inc(var_ready, 1)

            def norm_coefs(u):
                dve.wait_ge(rstd_ready, u + 1)
                mean, rstd = (rowsX[:, rows_of(u), D + i] for i in range(2))
                V.tensor_scalar(bcoef[:, rows_of(u), 0], rstd, 1.0, None, ALU.add)
                V.scalar_tensor_tensor(out=bcoef[:, rows_of(u), 1], in0=mean, scalar=-1.0, in1=rstd,
                                       op0=ALU.mult, op1=ALU.mult).then_inc(coef_ready, 1)

            def choose(b):
                dve.wait_ge(log_ready, (b + 1) * CH)
                mx, fm = rsm[:, 0, :], rsm[:, 2, :]

                def wide(v):
                    return v.unsqueeze(2).broadcast_to([P, CH, E])
                link(V.tensor_reduce(mx, logits[:], AX_X, ALU.max))
                V.tensor_tensor(lwork[:, 0], logits[:], wide(mx), ALU.subtract).then_inc(lexp_in, 1)
                dve.wait_ge(lexp_in, b + 1)
                link(V.scalar_tensor_tensor(out=lwork[:, 2], in0=lwork[:, 0], scalar=0.0,
                                            in1=rev.unsqueeze(1).broadcast_to([P, CH, E]), op0=ALU.is_ge, op1=ALU.mult))
                link(V.tensor_reduce(fm, lwork[:, 2], AX_X, ALU.max))
                link(V.tensor_tensor(hot[:, b], lwork[:, 2], wide(fm), ALU.is_equal))
                V.engine_nop().then_inc(hot_ready, 1)
                V.tensor_scalar(rsm[:, 5, :], fm, -float(C), float(E * C), ALU.mult, ALU.add)

            def gate_of(b):
                g3 = rsm[:, 1, :]
                dve.wait_ge(lexp_ready, b + 1)
                link(V.tensor_reduce(g3, lwork[:, 1], AX_X, ALU.add))
                link(V.reciprocal(rowsX[:, b * CH:(b + 1) * CH, D + 2], g3))

            def place(b):
                pos, over, sl, first_slot = (rsm[:, i, :] for i in (3, 4, 6, 5))
                dve.wait_ge(cnt_done, b + 1)
                V.tensor_tensor(lwork[:, 3], cnt_ps.rearrange("p (t e) -> p t e", t=CH), hot[:, b],
                                ALU.mult).then_inc(cnt_read, 1)
                dve.wait_ge(cnt_read, b + 1)
                link(V.tensor_reduce(pos, lwork[:, 3], AX_X, ALU.add))
                V.tensor_tensor(sl, first_slot, pos, ALU.add)
                link(V.tensor_scalar(over, pos, float(C), float(2 * SLOTS), ALU.is_ge, ALU.mult))
                V.tensor_tensor(slot[:, b * CH:(b + 1) * CH], sl, over, ALU.add).then_inc(slot_ready, 1)
                if b + 1 < B:
                    with nc.allow_low_precision(reason="counts up to 16 are exact in bfloat16"):
                        link(V.tensor_reduce(hotpart[:], hot[:, b].rearrange("p t e -> p e t"), AX_X, ALU.add))
                    link(V.tensor_tensor(hotsum[:], hotsum[:], hotpart[:], ALU.add))

            dve.wait_ge(cstb_set, 3)
            scaled_values(0)
            for s in range(NT):
                if s > CHOSEN and (s - CHOSEN - 1) % CH == 0:
                    gate_of((s - CHOSEN - 1) // CH)
                    place((s - CHOSEN - 1) // CH)
                decay_scores(s)
                if s + 1 == HN:
                    dve.wait_ge(tok_ready, 2)
                    dve.wait_ge(chdec_ready, 2)
                if s + 1 < NT and (s + 1) % CH < CH - 1:
                    scaled_values(s + 1)
                if s >= CHOSEN and (s - CHOSEN) % CH == 0:
                    choose((s - CHOSEN) // CH)
                if s % CH < CH - 1:
                    update_state(s)
                if s >= 1:
                    combine(s - 1)
                if s % 2 == 0 and s >= 2:
                    normalizer((s - 2) // 2)
                if s % 2 == 0 and s >= 4:
                    norm_coefs((s - 4) // 2)
                if s == NT - 1:
                    normalizer(PAIRS)
                if s % 2 == 1 and s >= 3:
                    residual((s - 3) // 2)
                if s == 0:
                    add_bias(1)
                if s == 1:
                    sum_log_forget(1)
                if s == 2:
                    running_max(1)
                    exp_arguments(1)
                if s == 3:
                    select_decays(1)
                if s == 4:
                    copy_decays(1)
            combine(NT - 1)
            normalizer(PAIRS + 1)
            norm_coefs(PAIRS - 1)
            residual(PAIRS)
            residual(PAIRS + 1)
            norm_coefs(PAIRS)
            norm_coefs(PAIRS + 1)
            choose(B - 2)
            gate_of(B - 2)
            place(B - 2)
            choose(B - 1)
            gate_of(B - 1)
            place(B - 1)

            def e_norm(e):
                if e % 4 == 0:
                    dve.wait_ge(erow_in[e // 4 % 4], 16 * (e // NR + 1))
                if e >= 2:
                    dve.wait_ge(e_xtT_done, e - 1)
                    dve.wait_ge(e_base, e - 1)
                r = erow[0:C, e % NR, :]
                V.tensor_scalar(ext[0:C, e % 2, :], r[:, 0:D], r[:, D:D + 1], r[:, D + 1:D + 2],
                                ALU.subtract, ALU.mult).then_inc(e_xt, 1)

            def e_evac(e):
                dve.wait_ge(e_xtT_done, e + 1)
                if e >= 2:
                    dve.wait_ge(e_gu, e - 1)
                V.tensor_copy(extT[:, e % 2, :, 0:C], (pown, pearly)[e % 2][:, 0:G * C].rearrange(
                    "p (g c) -> p g c", g=G)).then_inc(e_xtT, 1)

            def e_mul(e):
                dve.wait_ge(e_sil, e + 1)
                if e >= 2:
                    dve.wait_ge(e_y, e - 1)
                V.tensor_tensor(ehT[:, e % 2],
                                pq[:, e % 2, G * CW:2 * G * CW].rearrange("p (g c) -> p g c", g=G)[:, :, 0:C],
                                esil[:, e % 2], ALU.mult).then_inc(e_h, 1)

            def e_combine(e):
                dve.wait_ge(e_y, e + 1)
                dve.wait_ge(e_base, e + 1)
                if e >= 4:
                    dve.wait_ge(e_stored[e % 4], 16 * (e // 4))
                V.scalar_tensor_tensor(out=eout[0:C, e % 4, :], in0=pq[0:C, 2 + e % 2, 0:D],
                                       scalar=erow[0:C, e % NR, D + 2:D + 3], in1=ebase[0:C, e % 4, :],
                                       op0=ALU.mult, op1=ALU.add).then_inc(e_out, 1)

            dve.wait_ge(own_done, NT)
            V.memset(extT[:, :, :, C:CW], 0.0).then_inc(e_pad, 1)
            e_norm(0)
            e_evac(0)
            e_norm(1)
            for e in range(E):
                if e + 1 < E:
                    e_evac(e + 1)
                if e + 2 < E:
                    e_norm(e + 2)
                e_mul(e)
                if e >= 1:
                    e_combine(e - 1)
            e_combine(E - 1)


_INS = ['x', 'ctx_1024', 'L0_xattn_igate_kernel', 'L0_xattn_igate_bias', 'L0_xattn_fgate_kernel',
        'L0_xattn_fgate_bias', 'L0_ffn_w_router', 'L0_ffn_w_gate', 'L0_ffn_w_up', 'L0_ffn_w_down']


def shape_constants(B, D, NH, E):
    import numpy as np
    HD = D // NH
    G, HG, H1 = D // P, P // HD, HD + 1
    R = B * NH
    p = np.arange(P)
    ident = np.eye(P)
    head = np.repeat(np.arange(HG), H1)
    blockmask = np.tile((p[:, None] // HD == head[None, :]) * HD ** -0.5, (1, G))
    r = p - R
    headrow = (r[:, None] % HG == p[None, :] // HD) * 1.0
    bgmask = (r[:, None] // HG == np.arange(B * G)[None, :]) * 1.0
    rev = np.tile(E - np.arange(E), (P, 1))
    before = (p[:, None] < p[None, :]) * 1.0
    return np.concatenate([ident, blockmask, headrow, bgmask, rev, before, np.ones((P, P)),
                           np.full((P, 2 * NH), -0.5)], axis=1).astype(np.float32)


def kernel(**inputs):
    import numpy as _np
    import concourse.bacc as _bacc
    from concourse import mybir as _mybir
    from concourse.bass_utils import run_bass_kernel_spmd as _run

    nc = _bacc.Bacc("TRN2", target_bir_lowering=False, num_devices=1)
    arrays, args = {}, []
    for name in _INS:
        a = _np.ascontiguousarray(inputs[name])
        arrays[f"in_{name}_dram"] = a
        args.append(nc.dram_tensor(f"in_{name}_dram", a.shape, _mybir.dt.from_np(a.dtype), kind="ExternalInput").ap())
    b, s, d = inputs['x'].shape
    c = shape_constants(b, d, inputs['L0_xattn_igate_kernel'].shape[1], inputs['L0_ffn_w_gate'].shape[0])
    arrays["in_consts_dram"] = c
    args.append(nc.dram_tensor("in_consts_dram", c.shape, _mybir.dt.from_np(c.dtype), kind="ExternalInput").ap())
    args.append(nc.dram_tensor("out_0_dram", (b, s, d), _mybir.dt.float32, kind="ExternalOutput").ap())
    build(nc, *args)
    r = _run(nc, [arrays], core_ids=[0])
    return r.results[0]["out_0_dram"]
```
